# Optimizing a Trainium2 kernel written in Bass

```python
import numpy as np
import jax
import jax.numpy as jnp

def _softmax(x, axis=-1):
    return jax.nn.softmax(x, axis=axis)

def _gelu(x):
    return jax.nn.gelu(x, approximate=True)

def _silu(x):
    return jax.nn.silu(x)

def _sigmoid(x):
    return jax.nn.sigmoid(x)

def _layernorm(x, axis=-1, eps=1e-05):
    m = jnp.mean(x, axis=axis, keepdims=True)
    v = jnp.var(x, axis=axis, keepdims=True)
    return (x - m) / jnp.sqrt(v + eps)

def _scatter_add(tgt, idx, src, axis=0):
    return tgt.at[idx].add(src)

def _segment_sum(src, seg, n):
    return jax.ops.segment_sum(src, seg, n)
kernel_name = 'mk_gnn_preln_d4_gnn_r8_76e3e1'

def setup_inputs(seed: int=0):
    np.random.seed(seed)
    _w = jnp.asarray

    def _rec_inputs():
        import jax
        import jax.numpy as jnp
        _gk = jax.random.key(seed)
        x = -0.000202 + 1 * jax.random.normal(jax.random.fold_in(_gk, 1), (6250, 128), jnp.float32)
        src = jax.random.randint(jax.random.fold_in(_gk, 2), (200000,), 0, 6250, jnp.int32)
        dst = jax.random.randint(jax.random.fold_in(_gk, 3), (200000,), 0, 6250, jnp.int32)
        _o = jnp.argsort(dst, stable=True)
        src = src[_o]
        dst = dst[_o]
        edge_attr_64 = 0.000167468 + 1.0002 * jax.random.normal(jax.random.fold_in(_gk, 12), (200000, 64), jnp.float32)
        return (x, src, dst, edge_attr_64)
    x, src, dst, edge_attr_64 = _rec_inputs()

    def _L0_gnn_setup():
        import jax, jax.numpy as jnp
        import numpy as np
        N_NODES = 6250
        N_EDGES = 80000
        D_IN = 128
        D_HID = 128
        GIN_EPS = 0.0
        BN_EPS = 1e-05
        key = jax.random.key(seed)
        k = jax.random.split(key, 8)
        x = jax.random.normal(k[0], (N_NODES, D_IN), dtype=jnp.float32)
        edge_index = jax.random.randint(k[1], (2, N_EDGES), 0, N_NODES, dtype=jnp.int64)
        s1 = 1.0 / np.sqrt(D_IN)
        s2 = 1.0 / np.sqrt(D_HID)
        W1 = jax.random.uniform(k[2], (D_IN, D_HID), jnp.float32, -s1, s1)
        b1 = jax.random.uniform(k[3], (D_HID,), jnp.float32, -s1, s1)
        W2 = jax.random.uniform(k[4], (D_HID, D_HID), jnp.float32, -s2, s2)
        b2 = jax.random.uniform(k[5], (D_HID,), jnp.float32, -s2, s2)
        gamma = jnp.ones((D_HID,), jnp.float32)
        beta = jnp.zeros((D_HID,), jnp.float32)
        return {'x': x, 'edge_index': edge_index, 'W1': W1, 'b1': b1, 'W2': W2, 'b2': b2, 'gamma': gamma, 'beta': beta}
    _L0_gnn_all = _L0_gnn_setup()
    _L0_gnn_in = {k: v for k, v in _L0_gnn_all.items() if k in ('W1', 'b1', 'W2', 'b2', 'gamma', 'beta')}
    del _L0_gnn_all

    def _L1_gnn_setup():
        import jax, jax.numpy as jnp
        import numpy as np
        N_NODES = 12500
        NEG_SLOPE = 0.2
        key = jax.random.key(seed)
        k1, k2, k3, k4, k5 = jax.random.split(key, 5)
        N, E, Fin, Fout = (N_NODES, 400000, 128, 128)
        x = jax.random.normal(k1, (N, Fin), dtype=jnp.float32)
        edge_index = jax.random.randint(k2, (2, E), 0, N, dtype=jnp.int64)
        limit = float(np.sqrt(6.0 / (Fin + Fout)))
        W = jax.random.uniform(k3, (Fin, Fout), jnp.float32, -limit, limit)
        alim = float(np.sqrt(6.0 / (1 + Fout)))
        att_src = jax.random.uniform(k4, (Fout,), jnp.float32, -alim, alim)
        att_dst = jax.random.uniform(k5, (Fout,), jnp.float32, -alim, alim)
        bias = jnp.zeros((Fout,), jnp.float32)
        return {'x': x, 'edge_index': edge_index, 'W': W, 'att_src': att_src, 'att_dst': att_dst, 'bias': bias}
    _L1_gnn_all = _L1_gnn_setup()
    _L1_gnn_in = {k: v for k, v in _L1_gnn_all.items() if k in ('W', 'att_src', 'att_dst', 'bias')}
    del _L1_gnn_all

    def _L2_gnn_setup():
        import jax, jax.numpy as jnp
        import numpy as np
        N_NODES = 6250
        N_EDGES = 75000
        HIDDEN = 128

        def _sage_conv(x, src, dst, W_l, W_r, b):
            msg = x[src]
            agg = jax.ops.segment_sum(msg, dst, num_segments=N_NODES)
            cnt = jax.ops.segment_sum(jnp.ones((src.shape[0],), x.dtype), dst, num_segments=N_NODES)
            mean = agg / jnp.maximum(cnt, 1.0)[:, None]
            return mean @ W_l.T + x @ W_r.T + b
        key = jax.random.key(seed)
        ks = jax.random.split(key, 12)
        x = jax.random.normal(ks[0], (N_NODES, HIDDEN), dtype=jnp.float32)
        edge_index = jax.random.randint(ks[1], (2, N_EDGES), 0, N_NODES, dtype=jnp.int64)
        scale = 1.0 / np.sqrt(HIDDEN)
        inp = {'x': x, 'edge_index': edge_index}
        for i, layer in enumerate(['1', '2', '3']):
            inp['Wl' + layer] = jax.random.uniform(ks[2 + 3 * i], (HIDDEN, HIDDEN), minval=-scale, maxval=scale, dtype=jnp.float32)
            inp['Wr' + layer] = jax.random.uniform(ks[3 + 3 * i], (HIDDEN, HIDDEN), minval=-scale, maxval=scale, dtype=jnp.float32)
            inp['b' + layer] = jax.random.uniform(ks[4 + 3 * i], (HIDDEN,), minval=-scale, maxval=scale, dtype=jnp.float32)
        return inp
    _L2_gnn_all = _L2_gnn_setup()
    _L2_gnn_in = {k: v for k, v in _L2_gnn_all.items() if k in ('Wl1', 'Wr1', 'b1', 'Wl2', 'Wr2', 'b2', 'Wl3', 'Wr3', 'b3')}
    del _L2_gnn_all

    def _L3_gnn_setup():
        import jax, jax.numpy as jnp
        import numpy as np
        N_NODES = 5000
        N_EDGES = 80000
        N_GRAPHS = 64
        NODE_NF = 128
        EDGE_NF = 64
        GLOBAL_NF = 64
        HIDDEN_NF = 128
        key = jax.random.key(seed)
        ks = jax.random.split(key, 16)
        x = jax.random.normal(ks[0], (N_NODES, NODE_NF), dtype=jnp.float32)
        edge_index = jax.random.randint(ks[1], (2, N_EDGES), 0, N_NODES, dtype=jnp.int64)
        edge_attr = jax.random.normal(ks[2], (N_EDGES, EDGE_NF), dtype=jnp.float32)
        u = jax.random.normal(ks[3], (N_GRAPHS, GLOBAL_NF), dtype=jnp.float32)
        batch = jnp.sort(jax.random.randint(ks[4], (N_NODES,), 0, N_GRAPHS, dtype=jnp.int64))

        def lin(k, fin, fout):
            s = 1.0 / np.sqrt(fin)
            kw, kb = jax.random.split(k)
            W = jax.random.uniform(kw, (fin, fout), minval=-s, maxval=s, dtype=jnp.float32)
            b = jax.random.uniform(kb, (fout,), minval=-s, maxval=s, dtype=jnp.float32)
            return (W, b)
        W1a, b1a = lin(ks[5], NODE_NF + EDGE_NF, HIDDEN_NF)
        W1b, b1b = lin(ks[6], HIDDEN_NF, HIDDEN_NF)
        W2a, b2a = lin(ks[7], NODE_NF + HIDDEN_NF + GLOBAL_NF, HIDDEN_NF)
        W2b, b2b = lin(ks[8], HIDDEN_NF, NODE_NF)
        return {'x': x, 'edge_index': edge_index, 'edge_attr': edge_attr, 'u': u, 'batch': batch, 'W1a': W1a, 'b1a': b1a, 'W1b': W1b, 'b1b': b1b, 'W2a': W2a, 'b2a': b2a, 'W2b': W2b, 'b2b': b2b}
    _L3_gnn_all = _L3_gnn_setup()
    _L3_gnn_in = {k: v for k, v in _L3_gnn_all.items() if k in ('u', 'W1a', 'b1a', 'W1b', 'b1b', 'W2a', 'b2a', 'W2b', 'b2b')}
    del _L3_gnn_all
    return {'x': x, 'src': src, 'dst': dst, 'edge_attr_64': edge_attr_64, 'L0_gnn_W1': _L0_gnn_in['W1'], 'L0_gnn_b1': _L0_gnn_in['b1'], 'L0_gnn_W2': _L0_gnn_in['W2'], 'L0_gnn_b2': _L0_gnn_in['b2'], 'L0_gnn_gamma': _L0_gnn_in['gamma'], 'L0_gnn_beta': _L0_gnn_in['beta'], 'L1_gnn_W': _L1_gnn_in['W'], 'L1_gnn_att_src': _L1_gnn_in['att_src'], 'L1_gnn_att_dst': _L1_gnn_in['att_dst'], 'L1_gnn_bias': _L1_gnn_in['bias'], 'L2_gnn_Wl1': _L2_gnn_in['Wl1'], 'L2_gnn_Wr1': _L2_gnn_in['Wr1'], 'L2_gnn_b1': _L2_gnn_in['b1'], 'L2_gnn_Wl2': _L2_gnn_in['Wl2'], 'L2_gnn_Wr2': _L2_gnn_in['Wr2'], 'L2_gnn_b2': _L2_gnn_in['b2'], 'L2_gnn_Wl3': _L2_gnn_in['Wl3'], 'L2_gnn_Wr3': _L2_gnn_in['Wr3'], 'L2_gnn_b3': _L2_gnn_in['b3'], 'L3_gnn_u': _L3_gnn_in['u'], 'L3_gnn_W1a': _L3_gnn_in['W1a'], 'L3_gnn_b1a': _L3_gnn_in['b1a'], 'L3_gnn_W1b': _L3_gnn_in['W1b'], 'L3_gnn_b1b': _L3_gnn_in['b1b'], 'L3_gnn_W2a': _L3_gnn_in['W2a'], 'L3_gnn_b2a': _L3_gnn_in['b2a'], 'L3_gnn_W2b': _L3_gnn_in['W2b'], 'L3_gnn_b2b': _L3_gnn_in['b2b']}

def reference(x, src, dst, edge_attr_64, L0_gnn_W1, L0_gnn_b1, L0_gnn_W2, L0_gnn_b2, L0_gnn_gamma, L0_gnn_beta, L1_gnn_W, L1_gnn_att_src, L1_gnn_att_dst, L1_gnn_bias, L2_gnn_Wl1, L2_gnn_Wr1, L2_gnn_b1, L2_gnn_Wl2, L2_gnn_Wr2, L2_gnn_b2, L2_gnn_Wl3, L2_gnn_Wr3, L2_gnn_b3, L3_gnn_u, L3_gnn_W1a, L3_gnn_b1a, L3_gnn_W1b, L3_gnn_b1b, L3_gnn_W2a, L3_gnn_b2a, L3_gnn_W2b, L3_gnn_b2b):
    import jax
    import jax.numpy as jnp

    def _L0_gnn_ref(x, edge_index, W1, b1, W2, b2, gamma, beta):
        import jax, jax.numpy as jnp
        import numpy as np
        N_NODES = 6250
        N_EDGES = 80000
        D_IN = 128
        D_HID = 128
        GIN_EPS = 0.0
        BN_EPS = 1e-05
        src, dst = (edge_index[0], edge_index[1])
        agg = jax.ops.segment_sum(x[src], dst, num_segments=N_NODES)
        h = (1.0 + GIN_EPS) * x + agg
        h = jax.nn.relu(h @ W1 + b1)
        h = h @ W2 + b2
        h = jax.nn.relu(h)
        mean = jnp.mean(h, axis=0)
        var = jnp.var(h, axis=0)
        out = gamma * (h - mean) * jax.lax.rsqrt(var + BN_EPS) + beta
        return out

    def _L1_gnn_ref(x, edge_index, W, att_src, att_dst, bias):
        import jax, jax.numpy as jnp
        import numpy as np
        N_NODES = 12500
        NEG_SLOPE = 0.2
        N = x.shape[0]
        src, dst = (edge_index[0], edge_index[1])
        h = x @ W
        a_src = h @ att_src
        a_dst = h @ att_dst
        e = a_src[src] + a_dst[dst]
        e = jax.nn.leaky_relu(e, NEG_SLOPE)
        e_max = jax.ops.segment_max(e, dst, num_segments=N)
        e_max = jnp.where(jnp.isfinite(e_max), e_max, 0.0)
        e_exp = jnp.exp(e - e_max[dst])
        denom = jax.ops.segment_sum(e_exp, dst, num_segments=N)
        alpha = e_exp / (denom[dst] + 1e-16)
        out = jax.ops.segment_sum(alpha[:, None] * h[src], dst, num_segments=N)
        out = out + bias
        return jax.nn.relu(out)

    def _L2_gnn_ref(x, edge_index, Wl1, Wr1, b1, Wl2, Wr2, b2, Wl3, Wr3, b3):
        import jax, jax.numpy as jnp
        import numpy as np
        N_NODES = 6250
        N_EDGES = 75000
        HIDDEN = 128

        def _sage_conv(x, src, dst, W_l, W_r, b):
            msg = x[src]
            agg = jax.ops.segment_sum(msg, dst, num_segments=N_NODES)
            cnt = jax.ops.segment_sum(jnp.ones((src.shape[0],), x.dtype), dst, num_segments=N_NODES)
            mean = agg / jnp.maximum(cnt, 1.0)[:, None]
            return mean @ W_l.T + x @ W_r.T + b
        src, dst = (edge_index[0], edge_index[1])
        h = jax.nn.relu(_sage_conv(x, src, dst, Wl1, Wr1, b1))
        h = _sage_conv(h, src, dst, Wl2, Wr2, b2)
        h = _sage_conv(h, src, dst, Wl3, Wr3, b3)
        return h

    def _L3_gnn_ref(x, edge_index, edge_attr, u, batch, W1a, b1a, W1b, b1b, W2a, b2a, W2b, b2b):
        import jax, jax.numpy as jnp
        import numpy as np
        N_NODES = 5000
        N_EDGES = 80000
        N_GRAPHS = 64
        NODE_NF = 128
        EDGE_NF = 64
        GLOBAL_NF = 64
        HIDDEN_NF = 128
        row, col = (edge_index[0], edge_index[1])
        n_nodes = x.shape[0]
        h = jnp.concatenate([x[row], edge_attr], axis=1)
        h = jax.nn.relu(h @ W1a + b1a) @ W1b + b1b
        sums = jax.ops.segment_sum(h, col, num_segments=n_nodes)
        counts = jax.ops.segment_sum(jnp.ones((h.shape[0],), dtype=h.dtype), col, num_segments=n_nodes)
        agg = sums / jnp.clip(counts, 1.0)[:, None]
        z = jnp.concatenate([x, agg, u[batch]], axis=1)
        return jax.nn.relu(z @ W2a + b2a) @ W2b + b2b
    edge_index = jnp.stack([src, dst])
    batch0 = jnp.zeros((6250,), jnp.int32)
    h = jnp.maximum(_layernorm(x, axis=-1), 0.0)
    x = x + _L0_gnn_ref(h, edge_index, L0_gnn_W1, L0_gnn_b1, L0_gnn_W2, L0_gnn_b2, L0_gnn_gamma, L0_gnn_beta)
    h = jnp.maximum(_layernorm(x, axis=-1), 0.0)
    x = x + _L1_gnn_ref(h, edge_index, L1_gnn_W, L1_gnn_att_src, L1_gnn_att_dst, L1_gnn_bias)
    h = jnp.maximum(_layernorm(x, axis=-1), 0.0)
    x = x + _L2_gnn_ref(h, edge_index, L2_gnn_Wl1, L2_gnn_Wr1, L2_gnn_b1, L2_gnn_Wl2, L2_gnn_Wr2, L2_gnn_b2, L2_gnn_Wl3, L2_gnn_Wr3, L2_gnn_b3)
    h = jnp.maximum(_layernorm(x, axis=-1), 0.0)
    x = x + _L3_gnn_ref(h, edge_index, edge_attr_64, L3_gnn_u, batch0, L3_gnn_W1a, L3_gnn_b1a, L3_gnn_W1b, L3_gnn_b1b, L3_gnn_W2a, L3_gnn_b2a, L3_gnn_W2b, L3_gnn_b2b)
    return x

_drawn_inputs = setup_inputs


def setup_inputs(seed=0):
    import zlib

    import numpy as np

    out = dict(_drawn_inputs(seed))
    spreads = {'L0_gnn_gamma': (1.0, 0.2), 'L0_gnn_beta': (0.0, 0.277), 'L1_gnn_bias': (0.0, 0.389)}
    factors = {'edge_attr_64': 8.0,
     'L0_gnn_b1': 9.953,
     'L1_gnn_att_dst': 46.941,
     'L2_gnn_b1': 4.322,
     'L3_gnn_W1a': 8.0,
     'L3_gnn_b1a': 26.576,
     'L3_gnn_W1b': 5.031,
     'L3_gnn_b1b': 30.356,
     'L3_gnn_b2a': 5.991,
     'L0_gnn_b2': 2.792,
     'L1_gnn_att_src': 3.108,
     'L2_gnn_Wl1': 2.686,
     'L2_gnn_b2': 5.515,
     'L2_gnn_b3': 3.56,
     'L3_gnn_b2b': 4.38}
    for name, (base, spread) in spreads.items():
        noise = np.random.default_rng([zlib.crc32(name.encode()), seed]).standard_normal(out[name].shape)
        drawn = base * np.exp(spread * noise) if base else spread * noise
        out[name] = jnp.asarray(drawn.astype(out[name].dtype))
    for name, factor in factors.items():
        out[name] = (out[name] * factor).astype(out[name].dtype)
    return out
```

```python
import concourse.bass as bass
from concourse import mybir
from contextlib import ExitStack

P = 128
N_NODES, N_EDGES, D, D_EDGE = 6250, 200000, 128, 64
TILES = -(-N_NODES // P)
NODES = TILES * P
HALF, HALVES = 4, 2
BODY = HALF * HALVES
FULL_IN = N_EDGES // P
TAIL_IN = N_EDGES - FULL_IN * P
COLS_IN = FULL_IN + (TAIL_IN > 0)
CHUNKS = -(-(N_EDGES // P + TILES) // BODY) * BODY
ROUNDS = CHUNKS // BODY
EDGE_ROW = D + 2
ATT_ROW = D + 4
ROW = D + 4
BATCH = 7
BATCHES = TILES // BATCH
assert BATCH * BATCHES == TILES
EPS = 1e-5
SLOPE = 0.2

fp32, i32 = mybir.dt.float32, mybir.dt.int32
ALU = mybir.AluOpType
ACT = mybir.ActivationFunctionType
AX = mybir.AxisListType
ds = bass.ds


class Baton:

    def __init__(self, sem):
        self.sem, self.at = sem, 0


def relay(nc, baton, steps, rounds=1):
    start, length = baton.at, sum(inc for _, _, inc in steps)

    def program(name):
        def build(eng):
            def one_round(i):
                before = start
                for who, emit, inc in steps:
                    if who == name:
                        eng.wait_ge(baton.sem, i * length + before)
                        emit(eng, i).then_inc(baton.sem, inc)
                    before += inc
            if rounds == 1:
                one_round(0)
            else:
                with eng.Fori(0, rounds) as i:
                    one_round(i)
        return build

    with nc.Block() as block:
        on = {"sync": block.sync, "gpsimd": block.gpsimd, "vector": block.vector,
              "scalar": block.scalar, "tensor": block.tensor}
        for name in on:
            if any(who == name for who, _, _ in steps):
                on[name](program(name))
    baton.at = start + rounds * length


def build(nc, t, out):
    ctx = ExitStack()
    with ctx:
        def sb(name, shape, dt=fp32):
            return ctx.enter_context(nc.sbuf_tensor(name, shape, dt))

        def sem(name):
            return ctx.enter_context(nc.semaphore(name))

        def dram(name, shape, dt=fp32):
            return nc.dram_tensor(name, shape, dt, kind="Internal").ap()

        table = dram("table", (NODES, D))
        att_table = dram("att_table", (NODES, ATT_ROW))
        bucketed = dram("bucketed", (P * CHUNKS, EDGE_ROW))
        att_rows = dram("att_rows", (P, CHUNKS, ATT_ROW))
        bucketed_v = bucketed.rearrange("(p c) w -> p c w", p=P)

        x = sb("x", [P, TILES, D])
        h = sb("h", [P, TILES, D])
        sums = sb("sums", [P, TILES, ROW])
        wide = sb("wide", [P, TILES, D])
        wide2 = sb("wide2", [P, TILES, D])
        src_i = sb("src_i", [P, CHUNKS], i32)
        dst_f = sb("dst_f", [P, CHUNKS])
        tile_i = sb("tile_i", [1, CHUNKS], i32)
        a_src_e = sb("a_src_e", [P, CHUNKS])
        a_dst_e = sb("a_dst_e", [P, CHUNKS])
        ring = sb("ring", [P, HALVES, HALF, ROW])
        onehot = sb("onehot", [P, HALVES, HALF, P])
        extra = sb("extra", [P, HALVES, HALF, P])
        edge_in = sb("edge_in", [P, HALVES, HALF, D])
        idx = sb("idx", [P, HALVES, HALF], i32)
        junk = sb("junk", [P, P])
        stage = [sb(f"stage{k}", [P, BATCH, D]) for k in range(2)]
        turned = [sb(f"turned{k}", [P, BATCH, D]) for k in range(2)]
        ident = sb("ident", [P, P])
        ones = sb("ones", [P, P])
        before = sb("before", [P, P])
        iota = sb("iota", [P, P])
        eps = sb("eps", [P, 1])
        psum = ctx.enter_context(nc.psum_tensor("psum", [P, 8, 512], fp32))
        flat = psum[:, :, :].rearrange("p b n -> p (b n)")

        def batch_psum(k):
            return flat[:, 1024 * k:1024 * k + BATCH * D].rearrange("p (t n) -> p t n", t=BATCH)

        def half_psum(hf):
            return flat[:, 1024 * hf:1024 * hf + 1024].rearrange("p (c n) -> p c n", c=HALF)

        relay_baton = Baton(sem("relay"))
        s_gate = sem("s_gate")

        def run(steps, rounds=1):
            relay(nc, relay_baton, steps, rounds)

        def batch(view, i):
            return view[:, ds(i * BATCH, BATCH), :]

        W = {}
        loads = []
        for name in ("L0_gnn_W1", "L0_gnn_W2", "L1_gnn_W", "L2_gnn_Wl1", "L2_gnn_Wr1", "L2_gnn_Wl2", "L2_gnn_Wr2",
                     "L2_gnn_Wl3", "L2_gnn_Wr3", "L3_gnn_W1b", "L3_gnn_W2b"):
            W[name] = sb("w_" + name, [P, D])
            loads.append((W[name][:, :], t[name]))
        W["edge"] = sb("w_edge", [D_EDGE, D])
        W["u"] = sb("w_u", [D_EDGE, D])
        for name in ("node", "h", "agg"):
            W[name] = sb("w_" + name, [P, D])
        loads += [(W["node"][:, :], t["L3_gnn_W1a"][0:D, :]), (W["edge"][:, :], t["L3_gnn_W1a"][D:D + D_EDGE, :]),
                  (W["h"][:, :], t["L3_gnn_W2a"][0:D, :]), (W["agg"][:, :], t["L3_gnn_W2a"][D:2 * D, :]),
                  (W["u"][:, :], t["L3_gnn_W2a"][2 * D:2 * D + D_EDGE, :])]
        col = {}
        for name in ("L0_gnn_b1", "L0_gnn_b2", "L0_gnn_gamma", "L0_gnn_beta"):
            col[name] = sb("c_" + name, [P, 1])
            loads.append((col[name][:, :], t[name].rearrange("(f a) -> f a", a=1)))
        u0 = sb("u0", [D_EDGE, 1])
        loads.append((u0[:, :], t["L3_gnn_u"][0, :].rearrange("(f a) -> f a", a=1)))
        row = {}
        for name in ("L1_gnn_att_src", "L1_gnn_att_dst", "L1_gnn_bias", "L2_gnn_b1", "L2_gnn_b2", "L2_gnn_b3",
                     "L3_gnn_b1a", "L3_gnn_b1b", "L3_gnn_b2a", "L3_gnn_b2b"):
            row[name] = sb("r_" + name, [P, D])
            loads.append((row[name][:, :], t[name].partition_broadcast(P)))
        full_nodes = N_NODES // P
        loads += [(x[:, 0:full_nodes, :], t["x"][0:full_nodes * P, :].rearrange("(i p) f -> p i f", p=P)),
                  (x[0:N_NODES - full_nodes * P, full_nodes, :], t["x"][full_nodes * P:N_NODES, :])]

        def load_all(eng, _):
            for dst, src in loads[:-1]:
                eng.dma_start(dst, src).then_inc(s_load, 16)
            return eng.dma_start(*loads[-1])

        def part(tensor, at, n):
            whole = tensor[:, :, :].rearrange("p i w -> p (i w)")
            return whole[:, at:at + n]

        meta = part(h, 0, 2 * COLS_IN).rearrange("p (c w) -> p c w", w=2)
        slot_i = part(h, 3136, COLS_IN).bitcast(i32)
        tile_in = part(h, 4704, COLS_IN)
        tile_row = part(wide, 0, CHUNKS)
        chunk_no = part(wide, 2048, CHUNKS)
        dst_in = part(wide, 4096, COLS_IN).bitcast(i32)
        empty = part(wide2, 0, 16 * EDGE_ROW).rearrange("p (c w) -> p c w", c=16)
        src_in = part(wide2, 2112, COLS_IN).bitcast(i32)
        attr = part(wide2, 3712, BODY * P)[0:D_EDGE, :].rearrange("p (k n) -> p k n", k=HALVES)
        mask = part(sums, 0, COLS_IN).bitcast(i32)
        scan = part(sums, 2048, COLS_IN)
        slot = part(sums, 4096, COLS_IN)
        small = {n: sb("s_" + n, [P, TILES]) for n in
                 ("bucket", "partial", "count", "chunks", "ends", "start", "rcount", "some", "a_src", "a_dst",
                  "amax", "top", "mean", "rstd", "rden")}
        small_i = sb("small_i", [P, TILES], i32)
        moments = sb("moments", [P, TILES, 6])
        mean_var = sb("mean_var", [P, TILES, 2])

        s_load, s_tail, s_empty = sem("s_load"), sem("s_tail"), sem("s_empty")
        n_loads = len(loads)

        def consts_pool(e, _):
            e.memset(ident[:, :], 0.0)
            e.memset(before[:, :], 1.0)
            e.memset(dst_in, NODES)
            e.memset(src_in, 0)
            e.memset(empty, 0.0)
            e.memset(slot, 1.0)
            e.memset(ring[:, :, :, :], 0.0)
            e.memset(x[:, :, :], 0.0)
            e.iota(iota[:, :], [[1, P]], base=0, channel_multiplier=0, allow_small_or_imprecise_dtypes=True)
            e.iota(small["bucket"][:, :], [[1, TILES]], base=0, channel_multiplier=0,
                   allow_small_or_imprecise_dtypes=True)
            e.iota(chunk_no, [[1, CHUNKS]], base=0, channel_multiplier=0, allow_small_or_imprecise_dtypes=True)
            e.memset(ones[:, :], 1.0)
            e.memset(tile_row, -1.0)
            return e.memset(eps[:, :], EPS)

        def consts_pool2(e, _):
            e.affine_select(out=ident[:, :], in_=ident[:, :], compare_op=ALU.not_equal, fill=1.0, base=0,
                            pattern=[[-1, P]], channel_multiplier=1)
            e.affine_select(out=before[:, :], in_=before[:, :], compare_op=ALU.is_gt, fill=0.0, base=0,
                            pattern=[[1, P]], channel_multiplier=-1)
            e.memset(empty[:, :, D + 1:D + 2], -1.0)
            return e.memset(ring[:, :, :, D:D + 1], 1.0)

        def load_edges(e, _):
            e.dma_start(dst_in[:, 0:FULL_IN], t["dst_full"]).then_inc(s_tail, 16)
            e.dma_start(dst_in[0:TAIL_IN, FULL_IN:COLS_IN], t["dst_tail"]).then_inc(s_tail, 16)
            e.dma_start(src_in[:, 0:FULL_IN], t["src_full"]).then_inc(s_tail, 16)
            e.dma_start(src_in[0:TAIL_IN, FULL_IN:COLS_IN], t["src_tail"]).then_inc(s_tail, 16)
            e.dma_start(bucketed_v.rearrange("p (r c) w -> p r (c w)", c=16),
                        empty.rearrange("p c w -> p (c w)").unsqueeze(1).broadcast_to([P, CHUNKS // 16, 16 * EDGE_ROW])
                        ).then_inc(s_empty, 16)
            return load_all(e, _)

        def split_dst(e, _):
            e.wait_ge(s_tail, 64)
            e.wait_ge(s_load, 16 * (n_loads - 1))
            e.tensor_single_scalar(mask, dst_in, 7, op=ALU.arith_shift_right)
            return e.tensor_single_scalar(slot_i, dst_in, P - 1, op=ALU.bitwise_and)

        def to_float(e, _):
            e.tensor_copy(tile_in, mask)
            e.tensor_copy(meta[:, :, 0], src_in)
            return e.tensor_copy(meta[:, :, 1], slot_i)

        run([("gpsimd", consts_pool, 1), ("gpsimd", consts_pool2, 1), ("sync", load_edges, 16),
             ("vector", split_dst, 1), ("vector", to_float, 1)])

        def is_in_bucket(e, i):
            return e.tensor_scalar(mask, tile_in, small["bucket"][:, ds(i, 1)], None, op0=ALU.is_equal)

        def count_bucket(e, i):
            return e.tensor_reduce(small["partial"][:, ds(i, 1)], mask, axis=AX.X, op=ALU.add)

        run([("vector", is_in_bucket, 1), ("vector", count_bucket, 1)], TILES)

        s = small
        run([
            ("tensor", lambda e, _: e.matmul(flat[:, 0:TILES], lhsT=before[:, :], rhs=s["partial"][:, :], start=True, stop=True), 1),
            ("tensor", lambda e, _: e.matmul(flat[:, 512:512 + TILES], lhsT=ones[:, :], rhs=s["partial"][:, :], start=True, stop=True), 1),
            ("vector", lambda e, _: e.tensor_scalar(small_i[:, :], flat[:, 512:512 + TILES], float(P - 1), None, op0=ALU.add), 1),
            ("vector", lambda e, _: e.tensor_single_scalar(small_i[:, :], small_i[:, :], 7, op=ALU.arith_shift_right), 1),
            ("vector", lambda e, _: e.tensor_copy(s["chunks"][:, :], small_i[:, :]), 1),
            ("vector", lambda e, _: e.tensor_tensor_scan(s["ends"][:, :], ones[:, 0:TILES], s["chunks"][:, :], 0.0, ALU.mult, ALU.add), 1),
            ("vector", lambda e, _: e.tensor_tensor(s["ends"][:, :], s["ends"][:, :], s["chunks"][:, :], ALU.subtract), 1),
            ("vector", lambda e, _: e.scalar_tensor_tensor(s["start"][:, :], s["ends"][:, :], float(P), flat[:, 0:TILES], ALU.mult, ALU.add), 1),
        ])

        def rank(e, i):
            return e.tensor_tensor_scan(scan, mask, mask, s["start"][:, ds(i, 1)], ALU.add, ALU.max)

        def place(e, i):
            e.sem_inc(s_gate, 1)
            return e.copy_predicated(slot, mask, scan)

        def chunk_tile(e, i):
            return e.scalar_tensor_tensor(tile_row, chunk_no, s["ends"][:, ds(i, 1)], tile_row, ALU.is_ge, ALU.add)

        run([("vector", is_in_bucket, 1), ("vector", rank, 1), ("vector", place, 1), ("vector", chunk_tile, 1)], TILES)

        run([
            ("vector", lambda e, _: e.tensor_copy(tile_i[:, :], tile_row[0:1, :]), 1),
            ("vector", lambda e, _: e.tensor_scalar(mask, slot, -1.0, None, op0=ALU.add), 1),
            ("vector", lambda e, _: e.tensor_single_scalar(slot_i, mask, P - 1, op=ALU.bitwise_and), 1),
            ("vector", lambda e, _: e.tensor_single_scalar(mask, mask, 7, op=ALU.arith_shift_right), 1),
            ("vector", lambda e, _: e.scalar_tensor_tensor(slot_i, slot_i, float(CHUNKS), mask, ALU.mult, ALU.add), 1),
        ])

        def scatter_edges():
            in_rounds = FULL_IN // BODY
            s_attr = [sem(f"s_attr{k}") for k in range(HALVES)]
            s_mul = sem("s_mul")
            s_row = sem("s_row")
            s_meta = sem("s_meta")
            s_sent = [sem(f"s_sent{k}") for k in range(HALVES)]
            rest = FULL_IN - in_rounds * BODY

            with nc.Block() as block:
                @block.sync
                def _(e):
                    with e.Fori(0, in_rounds) as i:
                        for k in range(HALVES):
                            e.wait_ge(s_mul, 2 * i + k + 1)
                            e.dma_start(attr[:, k, :], t["attr_t"][:, ds((i * BODY + k * HALF) * P, HALF * P)]).then_inc(s_attr[k], 16)

                @block.tensor
                def _(e):
                    e.sem_inc(s_mul, 2)
                    with e.Fori(0, in_rounds) as i:
                        for k in range(HALVES):
                            e.wait_ge(s_attr[k], 16 * i + 16)
                            e.wait_ge(s_row, 4 * i + 2 * k + 2)
                            for c in range(HALF):
                                last = e.matmul(half_psum(k)[:, c, 0:D], lhsT=attr[:, k, c * P:(c + 1) * P],
                                                rhs=W["edge"][:, :], start=True, stop=True)
                            last.then_inc(s_mul, 1)

                @block.scalar
                def _(e):
                    e.sem_inc(s_row, 2 * HALVES)
                    with e.Fori(0, in_rounds) as i:
                        for k in range(HALVES):
                            e.wait_ge(s_sent[k], 16 * HALF * i)
                            e.wait_ge(s_mul, 2 * i + k + 3)
                            e.copy(ring[:, k, :, 0:D], half_psum(k)[:, :, 0:D]).then_inc(s_row, 1)
                            e.copy(idx[:, k, :], slot_i[:, ds(i * BODY + k * HALF, HALF)]).then_inc(s_row, 1)

                @block.vector
                def _(e):
                    with e.Fori(0, in_rounds) as i:
                        for k in range(HALVES):
                            e.wait_ge(s_sent[k], 16 * HALF * i)
                            e.tensor_copy(ring[:, k, :, D:D + 2], meta[:, ds(i * BODY + k * HALF, HALF), :]).then_inc(s_meta, 1)

                @block.gpsimd
                def _(e):
                    e.wait_ge(s_empty, 16)
                    with e.Fori(0, in_rounds) as i:
                        for k in range(HALVES):
                            e.wait_ge(s_row, 4 * i + 2 * k + 2 + 4)
                            e.wait_ge(s_meta, 2 * i + k + 1)
                            e.sem_inc(s_gate, 1)
                            for c in range(HALF):
                                e.indirect_dma_start(bucketed, bass.IndirectOffsetOnAxis(ap=idx[:, k, c:c + 1], axis=0),
                                                     ring[:, k, c, 0:EDGE_ROW], None).then_inc(s_sent[k], 16)
                    for k in range(HALVES):
                        e.wait_ge(s_sent[k], 16 * HALF * in_rounds)

            left = rest + (TAIL_IN > 0)
            sizes = [P] * rest + [TAIL_IN] * (TAIL_IN > 0)
            assert left <= HALF
            first = in_rounds * BODY
            s_left = sem("s_left")

            def send(e, _):
                for c, n in enumerate(sizes):
                    e.indirect_dma_start(bucketed, bass.IndirectOffsetOnAxis(ap=idx[0:n, 0, c:c + 1], axis=0),
                                         ring[0:n, 0, c, 0:EDGE_ROW], None).then_inc(s_left, 16)
                e.wait_ge(s_left, 16 * left)
                return e.nop()

            def multiply(e, _):
                for c, n in enumerate(sizes):
                    last = e.matmul(half_psum(0)[0:n, c, 0:D], lhsT=attr[:, 0, c * P:c * P + n], rhs=W["edge"][:, :], start=True, stop=True)
                return last

            def copy_terms(e, _):
                for c, n in enumerate(sizes):
                    last = e.copy(ring[0:n, 0, c, 0:D], half_psum(0)[0:n, c, 0:D])
                return last

            def copy_meta(e, _):
                e.tensor_copy(idx[:, 0, 0:left], slot_i[:, first:first + left])
                return e.tensor_copy(ring[:, 0, 0:left, D:D + 2], meta[:, first:first + left, :])

            n_left = N_EDGES - first * P
            run([("sync", lambda e, _: e.dma_start(attr[:, 0, 0:n_left], t["attr_t"][:, first * P:N_EDGES]), 16),
                 ("tensor", multiply, 1), ("scalar", copy_terms, 1), ("vector", copy_meta, 1), ("gpsimd", send, 1)])

        scatter_edges()

        def read_slots():
            s_in = [sem(f"s_in{k}") for k in range(HALVES)]
            s_cut = sem("s_cut")
            with nc.Block() as block:
                @block.sync
                def _(e):
                    with e.Fori(0, ROUNDS) as i:
                        for k in range(HALVES):
                            e.wait_ge(s_cut, 2 * i + k + 1)
                            e.dma_start(ring[:, k, :, 0:EDGE_ROW],
                                        bucketed_v[:, ds(i * BODY + k * HALF, HALF), :]).then_inc(s_in[k], 16)

                @block.vector
                def _(e):
                    e.sem_inc(s_cut, 2)
                    with e.Fori(0, ROUNDS) as i:
                        for k in range(HALVES):
                            e.wait_ge(s_in[k], 16 * i + 16)
                            e.tensor_copy(src_i[:, ds(i * BODY + k * HALF, HALF)], ring[:, k, :, D])
                            e.tensor_copy(dst_f[:, ds(i * BODY + k * HALF, HALF)], ring[:, k, :, D + 1]).then_inc(s_cut, 1)

            run([("gpsimd", lambda e, _: e.memset(ring[:, :, :, D:D + 1], 1.0), 1)])

        read_slots()

        def tiles(n=TILES):
            return [P, n, D]

        def layer_norm():
            def stats(e, i):
                for k in range(BATCH):
                    last = e.bn_stats(moments[:, ds(i * BATCH + k, 1), :].rearrange("p a s -> p (a s)"),
                                      x[:, ds(i * BATCH + k, 1), :].rearrange("p a f -> p (a f)"))
                return last
            run([("vector", stats, 1)], BATCHES)

            def aggregate(e, _):
                for k in range(TILES):
                    last = e.bn_aggr(mean_var[:, k, :], moments[:, k, :])
                return last
            mean, var = mean_var[:, :, 0], mean_var[:, :, 1]
            run([("vector", aggregate, 1),
                 ("scalar", lambda e, _: e.activation(s["rstd"][:, :], var, ACT.Sqrt, bias=eps[:, :]), 1),
                 ("vector", lambda e, _: e.reciprocal(s["rstd"][:, :], s["rstd"][:, :]), 1),
                 ("vector", lambda e, _: e.tensor_tensor(h[:, :, :], x[:, :, :], mean.unsqueeze(2).broadcast_to(tiles()), ALU.subtract), 1),
                 ("vector", lambda e, _: e.tensor_tensor(h[:, :, :], h[:, :, :], s["rstd"][:, :].unsqueeze(2).broadcast_to(tiles()), ALU.mult), 1),
                 ("scalar", lambda e, _: e.activation(h[:, :, :], h[:, :, :], ACT.Relu), 1)])

        def write_table(view):
            run([("sync", lambda e, _: e.dma_start(table.rearrange("(i p) f -> p i f", p=P), view), 16)])

        def turn(buffer, k):
            def emit(e, _):
                for c in range(BATCH):
                    last = e.transpose(batch_psum(k)[:, c, :], buffer[:, c, :], ident[:, :])
                return last
            return emit

        def dense(inputs, finish):
            steps = [("vector", lambda e, i: inputs[0][0](e, i, stage[0]), 1)]
            if len(inputs) > 1:
                steps.append(("vector", lambda e, i: inputs[1][0](e, i, stage[1]), 1))
            for k in range(len(inputs)):
                steps.append(("tensor", turn(stage[k], k), 1))
            for k, who in zip(range(len(inputs)), ("scalar", "vector")):
                copy = (lambda e, i, k=k: e.copy(turned[k][:, :, :], batch_psum(k))) if who == "scalar" else \
                       (lambda e, i, k=k: e.tensor_copy(turned[k][:, :, :], batch_psum(k)))
                steps.append((who, copy, 1))

            def multiply(e, i):
                for c in range(BATCH):
                    for k, (_, w) in enumerate(inputs):
                        last = e.matmul(batch_psum(2)[:, c, :], lhsT=turned[k][:, c, :], rhs=w[:, :],
                                        start=k == 0, stop=k == len(inputs) - 1)
                return last
            steps.append(("tensor", multiply, 1))
            steps += [(who, (lambda e, i, f=f: f(e, i, batch_psum(2))), 1) for who, f in finish]
            run(steps, BATCHES)

        def from_nodes(view):
            return lambda e, i, out: e.tensor_copy(out[:, :, :], batch(view, i))

        def mean_of_sums(e, i, out):
            return e.tensor_tensor(out[:, :, :], batch(sums, i)[:, :, 0:D],
                                   s["rcount"][:, ds(i * BATCH, BATCH)].unsqueeze(2).broadcast_to(tiles(BATCH)), ALU.mult)

        def plus_row(name, dest):
            return lambda e, i, p: e.tensor_tensor(dest(i), p, row[name][:, :].unsqueeze(1).broadcast_to(tiles(BATCH)), ALU.add)

        def on_every_partition(column, dest):
            def diagonals(e, i):
                return e.tensor_tensor(stage[0][:, :, :], ident[:, :].unsqueeze(1).broadcast_to(tiles(BATCH)),
                                       column[:, ds(i * BATCH, BATCH)].unsqueeze(2).broadcast_to(tiles(BATCH)), ALU.mult)

            def spread(e, i):
                for c in range(BATCH):
                    last = e.matmul(batch_psum(0)[:, c, :], lhsT=ones[:, :], rhs=stage[0][:, c, :], start=True, stop=True)
                return last
            run([("vector", diagonals, 1), ("tensor", spread, 1),
                 ("vector", lambda e, i: e.tensor_copy(batch(dest, i), batch_psum(0)), 1)], BATCHES)

        def edge_pass(name, kind):
            s_idx = sem(name + "_idx")
            s_got = [sem(f"{name}_got{k}") for k in range(HALVES)]
            s_hot = sem(name + "_hot")
            s_msg = sem(name + "_msg")
            s_pre = sem(name + "_pre")
            s_pe = sem(name + "_pe")
            s_add = sem(name + "_add")
            s_side = [sem(f"{name}_side{k}") for k in range(HALVES)]
            s_seq = sem(name + "_seq")
            s_step = sem(name + "_step")
            s_exp = sem(name + "_exp")
            gathers = kind != "weigh"
            width = ATT_ROW if kind in ("max", "weigh") else D
            used = D if kind == "edge" else D + 1
            source = att_table if kind == "max" else table

            def cols(i, k, n=HALF):
                return ds(i * BODY + k * HALF, n)

            with nc.Block() as block:
                if gathers:
                    @block.gpsimd
                    def _(e):
                        with e.Fori(0, ROUNDS) as i:
                            for k in range(HALVES):
                                e.wait_ge(s_idx, 2 * i + k + 1)
                                e.wait_ge(s_pe if kind == "sum" else s_pre, 2 * i + k + 1)
                                if kind == "max":
                                    e.wait_ge(s_side[k], 16 * i)
                                e.sem_inc(s_gate, 1)
                                for c in range(HALF):
                                    e.indirect_dma_start(ring[:, k, c, 0:width], None, source,
                                                         bass.IndirectOffsetOnAxis(ap=idx[:, k, c:c + 1], axis=0)).then_inc(s_got[k], 16)

                if kind != "sum":
                    @block.sync
                    def _(e):
                        with e.Fori(0, ROUNDS) as i:
                            for k in range(HALVES):
                                if kind == "max":
                                    e.wait_ge(s_got[k], 16 * HALF * (i + 1))
                                    e.dma_start(att_rows[:, cols(i, k), :], ring[:, k, :, :]).then_inc(s_side[k], 16)
                                elif kind == "edge":
                                    e.wait_ge(s_pre, 2 * i + k + 1)
                                    e.dma_start(edge_in[:, k, :, :], bucketed_v[:, cols(i, k), 0:D]).then_inc(s_side[k], 16)
                                else:
                                    e.wait_ge(s_pe, 2 * i + k + 1)
                                    e.dma_start(ring[:, k, :, :], att_rows[:, cols(i, k), :]).then_inc(s_got[k], 16 * HALF)
                        if kind == "max":
                            for k in range(HALVES):
                                e.wait_ge(s_side[k], 16 * ROUNDS)

                @block.scalar
                def _(e):
                    with e.Fori(0, ROUNDS) as i:
                        for k in range(HALVES):
                            if gathers:
                                e.wait_ge(s_got[k], 16 * HALF * i)
                                e.copy(idx[:, k, :], src_i[:, cols(i, k)]).then_inc(s_idx, 1)
                            if kind == "edge" and k == 1:
                                for m in range(HALVES):
                                    e.wait_ge(s_pre, 2 * i + m + 3)
                                    e.activation(extra[:, m, :, :], extra[:, m, :, :], ACT.Relu).then_inc(s_msg, 1)
                            if kind == "weigh":
                                e.wait_ge(s_pre, 2 * i + k + 1)
                                e.activation(edge_w[:, k, :], edge_w[:, k, :], ACT.Exp).then_inc(s_exp, 1)
                                e.wait_ge(s_exp, 2 * i + k + 1)
                                e.wait_ge(s_pe, 2 * i + k + 1)
                                for c in range(HALF):
                                    last = e.activation(extra[:, k, c, :], onehot[:, k, c, :], ACT.Copy, scale=edge_w[:, k, c:c + 1])
                                last.then_inc(s_msg, 1)

                @block.tensor
                def _(e):
                    e.sem_inc(s_pe, 2)
                    with e.Fori(0, ROUNDS) as i:
                        for k in range(HALVES):
                            e.wait_ge(s_hot, 2 * i + k + 1)
                            e.wait_ge(s_add, 2 * i + k + 1)
                            if kind != "max":
                                e.wait_ge(s_got[k], 16 * HALF * (i + 1))
                            if kind != "sum":
                                e.wait_ge(s_msg, 2 * i + k + 1)
                            for c in range(HALF):
                                if kind == "max":
                                    last = e.matmul(half_psum(k)[:, c, 0:P], lhsT=onehot[:, k, c, :], rhs=extra[:, k, c, :], start=True, stop=True)
                                else:
                                    lhsT = extra[:, k, c, :] if kind == "weigh" else onehot[:, k, c, :]
                                    rhs = extra[:, k, c, :] if kind == "edge" else ring[:, k, c, 0:used]
                                    last = e.matmul(half_psum(k)[:, c, 0:used], lhsT=lhsT, rhs=rhs, start=True, stop=True)
                            last.then_inc(s_pe, 1)

                @block.vector
                def _(e):
                    e.sem_inc(s_add, 2)
                    if kind in ("max", "edge"):
                        e.sem_inc(s_pre, 2)

                    def hot(i, k):
                        e.wait_ge(s_pe, 2 * i + k + 1)
                        e.tensor_tensor(onehot[:, k, :, :], iota[:, :].unsqueeze(1).broadcast_to([P, HALF, P]),
                                        dst_f[:, cols(i, k)].unsqueeze(2).broadcast_to([P, HALF, P]), ALU.is_equal).then_inc(s_hot, 1)

                    def pre(i, k, tile):
                        if kind == "edge":
                            e.wait_ge(s_got[k], 16 * HALF * (i + 1))
                            e.wait_ge(s_side[k], 16 * (i + 1))
                            e.tensor_tensor(extra[:, k, :, :], ring[:, k, :, 0:D], edge_in[:, k, :, :], ALU.add).then_inc(s_pre, 1)
                        if kind == "max":
                            e.wait_ge(s_hot, 2 * i + k + 1)
                            for c in range(HALF):
                                last = e.scalar_tensor_tensor(edge_in[:, k, c, :], onehot[:, k, c, :], 1.0, wide[:, ds(tile[c], 1), :].rearrange("p a n -> p (a n)"),
                                                              ALU.mult, ALU.mult, accum_out=edge_w[:, k, c:c + 1])
                            last.then_inc(s_exp, 1)
                            e.wait_ge(s_exp, 2 * i + k + 1)
                            e.tensor_copy(a_dst_e[:, cols(i, k)], edge_w[:, k, :])
                            e.wait_ge(s_got[k], 16 * HALF * (i + 1))
                            e.tensor_copy(a_src_e[:, cols(i, k)], ring[:, k, :, D + 1])
                            e.tensor_tensor(extra[:, k, :, :], ident[:, :].unsqueeze(1).broadcast_to([P, HALF, P]),
                                            ring[:, k, :, D + 2:D + 3].broadcast_to([P, HALF, P]), ALU.mult).then_inc(s_msg, 1)
                            e.wait_ge(s_msg, 2 * i + k + 1)
                            e.sem_inc(s_pre, 1)
                        if kind == "weigh":
                            at = (2 * i + k) * 3
                            e.wait_ge(s_hot, 2 * i + k + 1)
                            for c in range(HALF):
                                last = e.scalar_tensor_tensor(edge_in[:, k, c, :], onehot[:, k, c, :], 1.0,
                                                              wide2[:, ds(tile[c], 1), :].rearrange("p a n -> p (a n)"),
                                                              ALU.mult, ALU.mult, accum_out=edge_m[:, c:c + 1])
                            e.tensor_tensor(edge_z[:, :], a_src_e[:, cols(i, k)], a_dst_e[:, cols(i, k)], ALU.add).then_inc(s_step, 1)
                            e.wait_ge(s_step, at + 1)
                            e.scalar_tensor_tensor(edge_y[:, :], edge_z[:, :], SLOPE, edge_z[:, :], ALU.mult, ALU.max).then_inc(s_step, 1)
                            e.wait_ge(s_step, at + 2)
                            e.tensor_tensor(edge_w[:, k, :], edge_y[:, :], edge_m[:, :], ALU.subtract).then_inc(s_step, 1)
                            e.wait_ge(s_step, at + 3)
                            e.sem_inc(s_pre, 1)

                    def add(i, k, tile):
                        e.wait_ge(s_pe, 2 * i + k + 3)
                        at = (2 * i + k) * HALF
                        if kind == "max":
                            e.tensor_reduce(edge_z[:, :], half_psum(k)[:, :, 0:P], axis=AX.X, op=ALU.max).then_inc(s_idx2, 1)
                            e.wait_ge(s_idx2, 2 * i + k + 1)
                        for c in range(HALF):
                            if kind == "max":
                                to = s["amax"][:, ds(tile[c], 1)]
                                e.tensor_tensor(to, to, edge_z[:, c:c + 1], ALU.max).then_inc(s_seq, 1)
                            else:
                                to = sums[:, ds(tile[c], 1), 0:used].rearrange("p a n -> p (a n)")
                                e.tensor_tensor(to, to, half_psum(k)[:, c, 0:used], ALU.add).then_inc(s_seq, 1)
                            e.wait_ge(s_seq, at + c + 1)
                        e.sem_inc(s_add, 1)

                    with e.Fori(0, ROUNDS) as i:
                        tile = [[e.value_load(tile_i[0:1, ds(i * BODY + k * HALF + c, 1)], min_val=0, max_val=TILES - 1)
                                 for c in range(HALF)] for k in range(HALVES)]
                        for k in range(HALVES):
                            hot(i, k)
                        for k in range(HALVES):
                            pre(i, k, tile[k])
                        for k in range(HALVES):
                            add(i, k, tile[k])

        edge_w = sb("edge_w", [P, HALVES, HALF])
        edge_z, edge_y, edge_m = (sb(n, [P, HALF]) for n in ("edge_z", "edge_y", "edge_m"))
        s_idx2 = sem("s_reduced")

        def zero_sums():
            run([("vector", lambda e, _: e.memset(sums[:, :, :], 0.0), 1)])

        layer_norm()
        write_table(h[:, :, :])
        zero_sums()
        edge_pass("gin", "sum")
        counts = sums[:, :, D]
        run([("vector", lambda e, _: e.tensor_scalar(s["rcount"][:, :], counts, 1.0, None, op0=ALU.max), 1),
             ("vector", lambda e, _: e.reciprocal(s["rcount"][:, :], s["rcount"][:, :]), 1),
             ("vector", lambda e, _: e.tensor_tensor(s["some"][:, :], s["rcount"][:, :], counts, ALU.mult), 1)])
        by_feature = wide[:, :, :].rearrange("p i n -> p (i n)")
        split = BATCH * D // 2

        def mlp_product(w, k):
            def emit(e, i):
                src = turned[0][:, :, :].rearrange("p t n -> p (t n)") if k == 1 else stage[1][:, :, :].rearrange("p t n -> p (t n)")
                for m in range(2):
                    last = e.matmul(psum[:, 2 * k + m, 0:split], lhsT=w[:, :], rhs=src[:, m * split:(m + 1) * split], start=True, stop=True)
                return last
            return emit

        def halves(view):
            return view.rearrange("p (m n) -> p m n", m=2)
        run([
            ("vector", lambda e, i: e.tensor_tensor(stage[0][:, :, :], batch(h, i), batch(sums, i)[:, :, 0:D], ALU.add), 1),
            ("tensor", turn(stage[0], 0), 1),
            ("scalar", lambda e, i: e.copy(turned[0][:, :, :], batch_psum(0)), 1),
            ("tensor", mlp_product(W["L0_gnn_W1"], 1), 1),
            ("scalar", lambda e, i: e.activation(halves(stage[1][:, :, :].rearrange("p t n -> p (t n)")), psum[:, 2:4, 0:split], ACT.Relu,
                                                 bias=col["L0_gnn_b1"][:, :]), 1),
            ("tensor", mlp_product(W["L0_gnn_W2"], 2), 1),
            ("scalar", lambda e, i: e.activation(halves(by_feature[:, ds(i * BATCH * D, BATCH * D)]), psum[:, 4:6, 0:split], ACT.Relu,
                                                 bias=col["L0_gnn_b2"][:, :]), 1),
        ], BATCHES)
        pieces = [(a, min(512, N_NODES - a)) for a in range(0, N_NODES, 512)]

        def column_stats(e, _):
            for k, (a, n) in enumerate(pieces):
                last = e.bn_stats(moments[:, k, :], by_feature[:, a:a + n])
            return last
        scale_c, shift_c = sb("scale_c", [P, 1]), sb("shift_c", [P, 1])
        run([("vector", column_stats, 1),
             ("vector", lambda e, _: e.bn_aggr(mean_var[:, 0, :], moments[:, 0:len(pieces), :].rearrange("p k s -> p (k s)")), 1),
             ("scalar", lambda e, _: e.activation(scale_c[:, :], mean_var[:, 0, 1:2], ACT.Sqrt, bias=eps[:, :]), 1),
             ("vector", lambda e, _: e.reciprocal(scale_c[:, :], scale_c[:, :]), 1),
             ("vector", lambda e, _: e.tensor_tensor(scale_c[:, :], scale_c[:, :], col["L0_gnn_gamma"][:, :], ALU.mult), 1)])
        run([
            ("vector", lambda e, i: e.tensor_scalar(stage[0][:, :, :].rearrange("p t n -> p (t n)"), by_feature[:, ds(i * BATCH * D, BATCH * D)],
                                                    mean_var[:, 0, 0:1], scale_c[:, 0:1], op0=ALU.subtract, op1=ALU.mult), 1),
            ("scalar", lambda e, i: e.activation(stage[1][:, :, :], stage[0][:, :, :], ACT.Identity, bias=col["L0_gnn_beta"][:, :]), 1),
            ("tensor", turn(stage[1], 0), 1),
            ("vector", lambda e, i: e.tensor_tensor(batch(x, i), batch(x, i), batch_psum(0), ALU.add), 1),
        ], BATCHES)

        layer_norm()
        run([("vector", lambda e, _: e.memset(sums[:, :, D + 3:ROW], 0.0), 1)])

        def att(name, to):
            def product(e, i, p):
                return e.tensor_tensor(stage[1][:, :, :], batch(sums, i)[:, :, 0:D], row[name][:, :].unsqueeze(1).broadcast_to(tiles(BATCH)), ALU.mult)

            def total(e, i, p):
                return e.tensor_reduce(s[to][:, ds(i * BATCH, BATCH)], stage[1][:, :, :], axis=AX.X, op=ALU.add)
            return [("vector", product), ("vector", total)]
        dense([(from_nodes(h), W["L1_gnn_W"])],
              [("scalar", lambda e, i, p: e.copy(batch(sums, i)[:, :, 0:D], p))] + att("L1_gnn_att_src", "a_src") + att("L1_gnn_att_dst", "a_dst"))
        least, low = sb("least", [P, 1]), sb("low", [P, 1])
        run([("vector", lambda e, _: e.tensor_reduce(least[:, :], s["a_src"][:, :], axis=AX.X, op=ALU.min), 1),
             ("tensor", lambda e, _: e.transpose(flat[0:1, 0:P], least[:, :], ident[:, :]), 1),
             ("vector", lambda e, _: e.tensor_reduce(junk[0:1, 0:1], flat[0:1, 0:P], axis=AX.X, op=ALU.min), 1),
             ("tensor", lambda e, _: e.matmul(flat[:, 512:513], lhsT=ones[0:1, :], rhs=junk[0:1, 0:1], start=True, stop=True), 1),
             ("vector", lambda e, _: e.tensor_copy(low[:, :], flat[:, 512:513]), 1),
             ("vector", lambda e, _: e.memset(sums[:, :, D:D + 1], 1.0), 1),
             ("vector", lambda e, _: e.tensor_copy(sums[:, :, D + 1], s["a_src"][:, :]), 1),
             ("vector", lambda e, _: e.tensor_scalar(sums[:, :, D + 2], s["a_src"][:, :], low[:, 0:1], None, op0=ALU.subtract), 1),
             ("sync", lambda e, _: e.dma_start(att_table.rearrange("(i p) w -> p i w", p=P), sums[:, :, :]), 16),
             ("vector", lambda e, _: e.memset(s["amax"][:, :], 0.0), 1)])
        on_every_partition(s["a_dst"], wide)
        edge_pass("att_max", "max")
        run([("vector", lambda e, _: e.scalar_tensor_tensor(s["top"][:, :], s["amax"][:, :], low[:, 0:1], s["a_dst"][:, :], ALU.add, ALU.add), 1),
             ("vector", lambda e, _: e.scalar_tensor_tensor(s["mean"][:, :], s["top"][:, :], SLOPE, s["top"][:, :], ALU.mult, ALU.max), 1)])
        on_every_partition(s["mean"], wide2)
        zero_sums()
        edge_pass("att_sum", "weigh")
        run([("vector", lambda e, _: e.tensor_scalar(s["rden"][:, :], sums[:, :, D], 1e-16, None, op0=ALU.add), 1),
             ("vector", lambda e, _: e.reciprocal(s["rden"][:, :], s["rden"][:, :]), 1),
             ("vector", lambda e, _: e.tensor_tensor(h[:, :, :], sums[:, :, 0:D], s["rden"][:, :].unsqueeze(2).broadcast_to(tiles()), ALU.mult), 1),
             ("vector", lambda e, _: e.tensor_tensor(h[:, :, :], h[:, :, :], row["L1_gnn_bias"][:, :].unsqueeze(1).broadcast_to(tiles()), ALU.add), 1),
             ("vector", lambda e, _: e.scalar_tensor_tensor(x[:, :, :].rearrange("p i f -> p (i f)"), h[:, :, :].rearrange("p i f -> p (i f)"), 0.0,
                                                            x[:, :, :].rearrange("p i f -> p (i f)"), ALU.max, ALU.add), 1)])

        layer_norm()
        for n in (1, 2, 3):
            write_table(h[:, :, :])
            zero_sums()
            edge_pass(f"sage{n}", "sum")
            finish = [("vector", plus_row(f"L2_gnn_b{n}", lambda i: batch(h, i)))]
            if n == 1:
                finish.append(("scalar", lambda e, i, p: e.activation(batch(h, i), batch(h, i), ACT.Relu)))
            if n == 3:
                finish.append(("vector", lambda e, i, p: e.tensor_tensor(batch(x, i), batch(x, i), batch(h, i), ALU.add)))
            dense([(mean_of_sums, W[f"L2_gnn_Wl{n}"]), (from_nodes(h), W[f"L2_gnn_Wr{n}"])], finish)

        layer_norm()
        dense([(from_nodes(h), W["node"])], [("vector", plus_row("L3_gnn_b1a", lambda i: batch(wide, i)))])
        write_table(wide[:, :, :])
        zero_sums()
        edge_pass("meta", "edge")
        dense([(mean_of_sums, W["L3_gnn_W1b"])],
              [("vector", lambda e, i, p: e.tensor_tensor(stage[1][:, :, :], row["L3_gnn_b1b"][:, :].unsqueeze(1).broadcast_to(tiles(BATCH)),
                                                          s["some"][:, ds(i * BATCH, BATCH)].unsqueeze(2).broadcast_to(tiles(BATCH)), ALU.mult)),
               ("vector", lambda e, i, p: e.tensor_tensor(batch(wide, i), stage[1][:, :, :], p, ALU.add))])
        run([("vector", lambda e, _: e.tensor_copy(junk[0:D_EDGE, :], u0[:, :].broadcast_to([D_EDGE, P])), 1),
             ("tensor", lambda e, _: e.matmul(flat[:, 0:D], lhsT=junk[0:D_EDGE, :], rhs=W["u"][:, :], start=True, stop=True), 1),
             ("vector", lambda e, _: e.tensor_tensor(row["L3_gnn_b2a"][:, :], row["L3_gnn_b2a"][:, :], flat[:, 0:D], ALU.add), 1)])
        dense([(from_nodes(h), W["h"]), (from_nodes(wide), W["agg"])],
              [("vector", plus_row("L3_gnn_b2a", lambda i: batch(wide2, i))),
               ("scalar", lambda e, i, p: e.activation(batch(wide2, i), batch(wide2, i), ACT.Relu))])
        dense([(from_nodes(wide2), W["L3_gnn_W2b"])],
              [("vector", plus_row("L3_gnn_b2b", lambda i: batch(wide2, i))),
               ("vector", lambda e, i, p: e.tensor_tensor(batch(x, i), batch(x, i), batch(wide2, i), ALU.add))])
        s_out = sem("s_out")

        def store(e, _):
            e.dma_start(out[0:full_nodes * P, :].rearrange("(i p) f -> p i f", p=P), x[:, 0:full_nodes, :]).then_inc(s_out, 16)
            e.dma_start(out[full_nodes * P:N_NODES, :], x[0:N_NODES - full_nodes * P, full_nodes, :]).then_inc(s_out, 16)
            e.wait_ge(s_out, 32)
            return e.nop()
        run([("sync", store, 1)])


def kernel(**inputs):
    import numpy as np
    import concourse.bacc as bacc
    from concourse.bass_utils import run_bass_kernel_spmd as launch

    a = {k: np.ascontiguousarray(v) for k, v in inputs.items()}
    for n in (1, 2, 3):
        for side in "lr":
            a[f"L2_gnn_W{side}{n}"] = np.ascontiguousarray(a[f"L2_gnn_W{side}{n}"].T)
    for name in ("src", "dst"):
        v = a.pop(name)
        a[name + "_full"] = np.ascontiguousarray(v[:FULL_IN * P].reshape(FULL_IN, P).T)
        a[name + "_tail"] = np.ascontiguousarray(v[FULL_IN * P:].reshape(TAIL_IN, 1))
    a["attr_t"] = np.ascontiguousarray(a.pop("edge_attr_64").T)
    nc = bacc.Bacc("TRN2", target_bir_lowering=False, num_devices=1)
    t = {k: nc.dram_tensor("in_" + k, v.shape, mybir.dt.from_np(v.dtype), kind="ExternalInput").ap() for k, v in a.items()}
    out = nc.dram_tensor("out", (N_NODES, D), fp32, kind="ExternalOutput").ap()
    build(nc, t, out)
    r = launch(nc, [{"in_" + k: v for k, v in a.items()}], core_ids=[0])
    return r.results[0]["out"]
```

```python
import concourse.bass as bass
from concourse import mybir
from contextlib import ExitStack

P = 128
N_NODES, N_EDGES, D, D_EDGE = 6250, 200000, 128, 64
TILES = -(-N_NODES // P)
NODES = TILES * P
PAIR, SLOTS = 2, 4
BODY = PAIR * SLOTS
FULL_IN = N_EDGES // P
TAIL_IN = N_EDGES - FULL_IN * P
COLS_IN = FULL_IN + (TAIL_IN > 0)
PAIRS = -(-(N_EDGES // (PAIR * P) + TILES) // SLOTS) * SLOTS
CHUNKS = PAIRS * PAIR
ROUNDS = CHUNKS // BODY
EDGE_ROW = D + 2
ATT_ROW = D + 4
ROW = D + 4
BATCH = 7
BATCHES = TILES // BATCH
assert BATCH * BATCHES == TILES
EPS = 1e-5
SLOPE = 0.2

fp32, i32 = mybir.dt.float32, mybir.dt.int32
ALU = mybir.AluOpType
ACT = mybir.ActivationFunctionType
AX = mybir.AxisListType
ds = bass.ds


class Baton:

    def __init__(self, sem):
        self.sem, self.at = sem, 0


def relay(nc, baton, steps, rounds=1):
    start, length = baton.at, sum(inc for _, _, inc in steps)

    def program(name):
        def build(eng):
            def one_round(i):
                before = start
                for who, emit, inc in steps:
                    if who == name:
                        eng.wait_ge(baton.sem, i * length + before)
                        emit(eng, i).then_inc(baton.sem, inc)
                    before += inc
            if rounds == 1:
                one_round(0)
            else:
                with eng.Fori(0, rounds) as i:
                    one_round(i)
        return build

    with nc.Block() as block:
        on = {"sync": block.sync, "gpsimd": block.gpsimd, "vector": block.vector,
              "scalar": block.scalar, "tensor": block.tensor}
        for name in on:
            if any(who == name for who, _, _ in steps):
                on[name](program(name))
    baton.at = start + rounds * length


def rounds_of(eng, n, body, first=0, last=0):
    for i in range(first):
        body(i)
    with eng.Fori(first, n - last) as i:
        body(i)
    for i in range(n - last, n):
        body(i)


def build(nc, t, out):
    ctx = ExitStack()
    with ctx:
        def sb(name, shape, dt=fp32):
            return ctx.enter_context(nc.sbuf_tensor(name, shape, dt))

        def sem(name):
            return ctx.enter_context(nc.semaphore(name))

        def dram(name, shape, dt=fp32):
            return nc.dram_tensor(name, shape, dt, kind="Internal").ap()

        table = dram("table", (NODES, D))
        att_table = dram("att_table", (NODES, ATT_ROW))
        bucketed = dram("bucketed", (P * CHUNKS, EDGE_ROW))
        att_rows = dram("att_rows", (P, CHUNKS, ATT_ROW))
        bucketed_v = bucketed.rearrange("(p c) w -> p c w", p=P)

        x = sb("x", [P, TILES, D])
        h = sb("h", [P, TILES, D])
        sums = sb("sums", [P, TILES, ROW])
        wide = sb("wide", [P, TILES, D])
        wide2 = sb("wide2", [P, TILES, D])
        src_i = sb("src_i", [P, CHUNKS], i32)
        dst_f = sb("dst_f", [P, CHUNKS])
        tile_i = sb("tile_i", [1, PAIRS], i32)
        a_src_e = sb("a_src_e", [P, CHUNKS])
        a_dst_e = sb("a_dst_e", [P, CHUNKS])
        ring = sb("ring", [P, SLOTS, PAIR, ROW])
        onehot = sb("onehot", [P, SLOTS, PAIR, P])
        extra = sb("extra", [P, SLOTS, PAIR, P])
        edge_in = sb("edge_in", [P, SLOTS, PAIR, EDGE_ROW])
        idx = sb("idx", [P, SLOTS, PAIR], i32)
        junk = sb("junk", [P, P])
        stage = [sb(f"stage{k}", [P, BATCH, D]) for k in range(2)]
        turned = [sb(f"turned{k}", [P, BATCH, D]) for k in range(2)]
        ident = sb("ident", [P, P])
        ones = sb("ones", [P, P])
        before = sb("before", [P, P])
        iota = sb("iota", [P, P])
        eps = sb("eps", [P, 1])
        psum = ctx.enter_context(nc.psum_tensor("psum", [P, 8, 512], fp32))
        flat = psum[:, :, :].rearrange("p b n -> p (b n)")

        def batch_psum(k):
            return flat[:, 1024 * k:1024 * k + BATCH * D].rearrange("p (t n) -> p t n", t=BATCH)

        def pair_psum(k):
            return psum[:, k, :].rearrange("p (c n) -> p c n", c=PAIR)

        relay_baton = Baton(sem("relay"))
        s_gate = sem("s_gate")

        def run(steps, rounds=1):
            relay(nc, relay_baton, steps, rounds)

        def batch(view, i):
            return view[:, ds(i * BATCH, BATCH), :]

        W = {}
        loads = []
        for name in ("L0_gnn_W1", "L0_gnn_W2", "L1_gnn_W", "L2_gnn_Wl1", "L2_gnn_Wr1", "L2_gnn_Wl2", "L2_gnn_Wr2",
                     "L2_gnn_Wl3", "L2_gnn_Wr3", "L3_gnn_W1b", "L3_gnn_W2b"):
            W[name] = sb("w_" + name, [P, D])
            loads.append((W[name][:, :], t[name]))
        W["edge"] = sb("w_edge", [D_EDGE, D])
        W["u"] = sb("w_u", [D_EDGE, D])
        for name in ("node", "h", "agg"):
            W[name] = sb("w_" + name, [P, D])
        loads += [(W["node"][:, :], t["L3_gnn_W1a"][0:D, :]), (W["edge"][:, :], t["L3_gnn_W1a"][D:D + D_EDGE, :]),
                  (W["h"][:, :], t["L3_gnn_W2a"][0:D, :]), (W["agg"][:, :], t["L3_gnn_W2a"][D:2 * D, :]),
                  (W["u"][:, :], t["L3_gnn_W2a"][2 * D:2 * D + D_EDGE, :])]
        col = {}
        for name in ("L0_gnn_b1", "L0_gnn_b2", "L0_gnn_gamma", "L0_gnn_beta"):
            col[name] = sb("c_" + name, [P, 1])
            loads.append((col[name][:, :], t[name].rearrange("(f a) -> f a", a=1)))
        u0 = sb("u0", [D_EDGE, 1])
        loads.append((u0[:, :], t["L3_gnn_u"][0, :].rearrange("(f a) -> f a", a=1)))
        row = {}
        for name in ("L1_gnn_att_src", "L1_gnn_att_dst", "L1_gnn_bias", "L2_gnn_b1", "L2_gnn_b2", "L2_gnn_b3",
                     "L3_gnn_b1a", "L3_gnn_b1b", "L3_gnn_b2a", "L3_gnn_b2b"):
            row[name] = sb("r_" + name, [P, D])
            loads.append((row[name][:, :], t[name].partition_broadcast(P)))
        full_nodes = N_NODES // P
        loads += [(x[:, 0:full_nodes, :], t["x"][0:full_nodes * P, :].rearrange("(i p) f -> p i f", p=P)),
                  (x[0:N_NODES - full_nodes * P, full_nodes, :], t["x"][full_nodes * P:N_NODES, :])]

        def load_all(eng, _):
            for dst, src in loads[:-1]:
                eng.dma_start(dst, src).then_inc(s_load, 16)
            return eng.dma_start(*loads[-1])

        def part(tensor, at, n):
            whole = tensor[:, :, :].rearrange("p i w -> p (i w)")
            return whole[:, at:at + n]

        meta = part(h, 0, 2 * COLS_IN).rearrange("p (c w) -> p c w", w=2)
        slot_i = part(h, 3136, COLS_IN).bitcast(i32)
        tile_in = part(h, 4704, COLS_IN)
        tile_row = part(wide, 0, PAIRS)
        pair_no = part(wide, 2048, PAIRS)
        dst_in = part(wide, 4096, COLS_IN).bitcast(i32)
        empty = part(wide2, 0, 16 * EDGE_ROW).rearrange("p (c w) -> p c w", c=16)
        src_in = part(wide2, 2112, COLS_IN).bitcast(i32)
        attr = part(wide2, 3712, BODY * P)[0:D_EDGE, :].rearrange("p (k n) -> p k n", k=SLOTS)
        mask = part(sums, 0, COLS_IN).bitcast(i32)
        scan = part(sums, 2048, COLS_IN)
        slot = part(sums, 4096, COLS_IN)
        small = {n: sb("s_" + n, [P, TILES]) for n in
                 ("bucket", "partial", "count", "chunks", "ends", "start", "rcount", "some", "a_src", "a_dst",
                  "amax", "top", "mean", "rstd", "rden")}
        small_i = sb("small_i", [P, TILES], i32)
        moments = sb("moments", [P, TILES, 6])
        mean_var = sb("mean_var", [P, TILES, 2])

        s_load, s_tail, s_empty = sem("s_load"), sem("s_tail"), sem("s_empty")
        n_loads = len(loads)

        def consts_pool(e, _):
            e.memset(ident[:, :], 0.0)
            e.memset(before[:, :], 1.0)
            e.memset(dst_in, NODES)
            e.memset(src_in, 0)
            e.memset(empty, 0.0)
            e.memset(slot, 1.0)
            e.memset(ring[:, :, :, :], 0.0)
            e.memset(x[:, :, :], 0.0)
            e.iota(iota[:, :], [[1, P]], base=0, channel_multiplier=0, allow_small_or_imprecise_dtypes=True)
            e.iota(small["bucket"][:, :], [[1, TILES]], base=0, channel_multiplier=0,
                   allow_small_or_imprecise_dtypes=True)
            e.iota(pair_no, [[1, PAIRS]], base=0, channel_multiplier=0, allow_small_or_imprecise_dtypes=True)
            e.memset(ones[:, :], 1.0)
            e.memset(tile_row, -1.0)
            return e.memset(eps[:, :], EPS)

        def consts_pool2(e, _):
            e.affine_select(out=ident[:, :], in_=ident[:, :], compare_op=ALU.not_equal, fill=1.0, base=0,
                            pattern=[[-1, P]], channel_multiplier=1)
            e.affine_select(out=before[:, :], in_=before[:, :], compare_op=ALU.is_gt, fill=0.0, base=0,
                            pattern=[[1, P]], channel_multiplier=-1)
            e.memset(empty[:, :, D + 1:D + 2], -1.0)
            return e.memset(ring[:, :, :, D:D + 1], 1.0)

        def load_edges(e, _):
            e.dma_start(dst_in[:, 0:FULL_IN], t["dst_full"]).then_inc(s_tail, 16)
            e.dma_start(dst_in[0:TAIL_IN, FULL_IN:COLS_IN], t["dst_tail"]).then_inc(s_tail, 16)
            e.dma_start(src_in[:, 0:FULL_IN], t["src_full"]).then_inc(s_tail, 16)
            e.dma_start(src_in[0:TAIL_IN, FULL_IN:COLS_IN], t["src_tail"]).then_inc(s_tail, 16)
            return load_all(e, _)

        def fill_empty(e, _):
            e.dma_start(bucketed_v.rearrange("p (r c) w -> p r (c w)", c=16),
                        empty.rearrange("p c w -> p (c w)").unsqueeze(1).broadcast_to([P, CHUNKS // 16, 16 * EDGE_ROW])
                        ).then_inc(s_empty, 16)
            return e.nop()

        def split_dst(e, _):
            e.wait_ge(s_tail, 64)
            e.wait_ge(s_load, 16 * (n_loads - 1))
            e.tensor_single_scalar(mask, dst_in, 7, op=ALU.arith_shift_right)
            return e.tensor_single_scalar(slot_i, dst_in, P - 1, op=ALU.bitwise_and)

        def to_float(e, _):
            e.tensor_copy(tile_in, mask)
            e.tensor_copy(meta[:, :, 0], src_in)
            return e.tensor_copy(meta[:, :, 1], slot_i)

        run([("gpsimd", consts_pool, 1), ("gpsimd", consts_pool2, 1), ("sync", load_edges, 16),
             ("sync", fill_empty, 1), ("vector", split_dst, 1), ("vector", to_float, 1)])

        def is_in_bucket(e, i):
            return e.tensor_scalar(mask, tile_in, small["bucket"][:, ds(i, 1)], None, op0=ALU.is_equal)

        def count_bucket(e, i):
            return e.tensor_reduce(small["partial"][:, ds(i, 1)], mask, axis=AX.X, op=ALU.add)

        run([("vector", is_in_bucket, 1), ("vector", count_bucket, 1)], TILES)

        s = small
        run([
            ("tensor", lambda e, _: e.matmul(flat[:, 0:TILES], lhsT=before[:, :], rhs=s["partial"][:, :], start=True, stop=True), 1),
            ("tensor", lambda e, _: e.matmul(flat[:, 512:512 + TILES], lhsT=ones[:, :], rhs=s["partial"][:, :], start=True, stop=True), 1),
            ("vector", lambda e, _: e.tensor_scalar(small_i[:, :], flat[:, 512:512 + TILES], float(PAIR * P - 1), None, op0=ALU.add), 1),
            ("vector", lambda e, _: e.tensor_single_scalar(small_i[:, :], small_i[:, :], 8, op=ALU.arith_shift_right), 1),
            ("vector", lambda e, _: e.tensor_copy(s["chunks"][:, :], small_i[:, :]), 1),
            ("vector", lambda e, _: e.tensor_tensor_scan(s["ends"][:, :], ones[:, 0:TILES], s["chunks"][:, :], 0.0, ALU.mult, ALU.add), 1),
            ("vector", lambda e, _: e.tensor_tensor(s["ends"][:, :], s["ends"][:, :], s["chunks"][:, :], ALU.subtract), 1),
            ("vector", lambda e, _: e.scalar_tensor_tensor(s["start"][:, :], s["ends"][:, :], float(PAIR * P), flat[:, 0:TILES], ALU.mult, ALU.add), 1),
        ])

        def rank(e, i):
            return e.tensor_tensor_scan(scan, mask, mask, s["start"][:, ds(i, 1)], ALU.add, ALU.max)

        def place(e, i):
            e.sem_inc(s_gate, 1)
            return e.copy_predicated(slot, mask, scan)

        def chunk_tile(e, i):
            return e.scalar_tensor_tensor(tile_row, pair_no, s["ends"][:, ds(i, 1)], tile_row, ALU.is_ge, ALU.add)

        run([("vector", is_in_bucket, 1), ("vector", rank, 1), ("vector", place, 1), ("vector", chunk_tile, 1)], TILES)

        run([
            ("vector", lambda e, _: e.tensor_copy(tile_i[:, :], tile_row[0:1, :]), 1),
            ("vector", lambda e, _: e.tensor_scalar(mask, slot, -1.0, None, op0=ALU.add), 1),
            ("vector", lambda e, _: e.tensor_single_scalar(slot_i, mask, P - 1, op=ALU.bitwise_and), 1),
            ("vector", lambda e, _: e.tensor_single_scalar(mask, mask, 7, op=ALU.arith_shift_right), 1),
            ("vector", lambda e, _: e.scalar_tensor_tensor(slot_i, slot_i, float(CHUNKS), mask, ALU.mult, ALU.add), 1),
        ])

        def scatter_edges():
            in_rounds = FULL_IN // BODY
            s_attr = [sem(f"s_attr{k}") for k in range(SLOTS)]
            s_mul = sem("s_mul")
            s_row = sem("s_row")
            s_meta = sem("s_meta")
            s_sent = [sem(f"s_sent{k}") for k in range(SLOTS)]
            rest = FULL_IN - in_rounds * BODY

            def cols(i, k):
                return ds(i * BODY + k * PAIR, PAIR)

            with nc.Block() as block:
                @block.sync
                def _(e):
                    def one(i):
                        for k in range(SLOTS):
                            e.wait_ge(s_mul, SLOTS * i + k + 1)
                            e.dma_start(attr[:, k, :], t["attr_t"][:, ds((i * BODY + k * PAIR) * P, PAIR * P)]).then_inc(s_attr[k], 16)
                    rounds_of(e, in_rounds, one)

                @block.tensor
                def _(e):
                    e.sem_inc(s_mul, SLOTS)
                    def one(i):
                        for k in range(SLOTS):
                            e.wait_ge(s_attr[k], 16 * i + 16)
                            e.wait_ge(s_row, SLOTS * i + k + 1)
                            for c in range(PAIR):
                                last = e.matmul(pair_psum(k)[:, c, 0:D], lhsT=attr[:, k, c * P:(c + 1) * P],
                                                rhs=W["edge"][:, :], start=True, stop=True)
                            last.then_inc(s_mul, 1)
                    rounds_of(e, in_rounds, one)

                @block.scalar
                def _(e):
                    e.sem_inc(s_row, SLOTS)
                    def one(i):
                        for k in range(SLOTS):
                            e.wait_ge(s_sent[k], 16 * PAIR * i)
                            e.wait_ge(s_mul, SLOTS * i + k + 1 + SLOTS)
                            e.copy(idx[:, k, :], slot_i[:, cols(i, k)])
                            e.copy(ring[:, k, :, 0:D], pair_psum(k)[:, :, 0:D]).then_inc(s_row, 1)
                    rounds_of(e, in_rounds, one, first=1)

                @block.vector
                def _(e):
                    def one(i):
                        for k in range(SLOTS):
                            e.wait_ge(s_sent[k], 16 * PAIR * i)
                            e.tensor_copy(ring[:, k, :, D:D + 2], meta[:, cols(i, k), :]).then_inc(s_meta, 1)
                    rounds_of(e, in_rounds, one, first=1)

                @block.gpsimd
                def _(e):
                    e.wait_ge(s_empty, 16)
                    def one(i):
                        for k in range(SLOTS):
                            e.wait_ge(s_row, SLOTS * i + k + 1 + SLOTS)
                            e.wait_ge(s_meta, SLOTS * i + k + 1)
                            e.sem_inc(s_gate, 1)
                            for c in range(PAIR):
                                e.indirect_dma_start(bucketed, bass.IndirectOffsetOnAxis(ap=idx[:, k, c:c + 1], axis=0),
                                                     ring[:, k, c, 0:EDGE_ROW], None).then_inc(s_sent[k], 16)
                    rounds_of(e, in_rounds, one)
                    for k in range(SLOTS):
                        e.wait_ge(s_sent[k], 16 * PAIR * in_rounds)

            left = rest + (TAIL_IN > 0)
            sizes = [P] * rest + [TAIL_IN] * (TAIL_IN > 0)
            first = in_rounds * BODY
            n_left = N_EDGES - first * P
            s_left = sem("s_left")
            places = [(c // PAIR, c % PAIR, n) for c, n in enumerate(sizes)]

            def send(e, _):
                for k, c, n in places:
                    e.indirect_dma_start(bucketed, bass.IndirectOffsetOnAxis(ap=idx[0:n, k, c:c + 1], axis=0),
                                         ring[0:n, k, c, 0:EDGE_ROW], None).then_inc(s_left, 16)
                e.wait_ge(s_left, 16 * left)
                return e.nop()

            def multiply(e, _):
                for k, c, n in places:
                    last = e.matmul(pair_psum(k)[0:n, c, 0:D], lhsT=attr[:, k, c * P:c * P + n], rhs=W["edge"][:, :], start=True, stop=True)
                return last

            def copy_terms(e, _):
                for k, c, n in places:
                    last = e.copy(ring[0:n, k, c, 0:D], pair_psum(k)[0:n, c, 0:D])
                return last

            def copy_meta(e, _):
                for j, (k, c, _n) in enumerate(places):
                    e.tensor_copy(idx[:, k, c:c + 1], slot_i[:, first + j:first + j + 1])
                    last = e.tensor_copy(ring[:, k, c, D:D + 2], meta[:, first + j, :])
                return last

            run([("sync", lambda e, _: e.dma_start(part(wide2, 3712, n_left)[0:D_EDGE, :], t["attr_t"][:, first * P:N_EDGES]), 16),
                 ("tensor", multiply, 1), ("scalar", copy_terms, 1), ("vector", copy_meta, 1), ("gpsimd", send, 1),
                 ("gpsimd", lambda e, _: e.memset(ring[:, :, :, D:D + 1], 1.0), 1)])

        scatter_edges()

        def tiles(n=TILES):
            return [P, n, D]

        def layer_norm():
            def stats(e, i):
                for k in range(BATCH):
                    last = e.bn_stats(moments[:, ds(i * BATCH + k, 1), :].rearrange("p a s -> p (a s)"),
                                      x[:, ds(i * BATCH + k, 1), :].rearrange("p a f -> p (a f)"))
                return last
            run([("vector", stats, 1)], BATCHES)

            def aggregate(e, _):
                for k in range(TILES):
                    last = e.bn_aggr(mean_var[:, k, :], moments[:, k, :])
                return last
            mean, var = mean_var[:, :, 0], mean_var[:, :, 1]
            run([("vector", aggregate, 1),
                 ("scalar", lambda e, _: e.activation(s["rstd"][:, :], var, ACT.Sqrt, bias=eps[:, :]), 1),
                 ("vector", lambda e, _: e.reciprocal(s["rstd"][:, :], s["rstd"][:, :]), 1),
                 ("vector", lambda e, _: e.tensor_tensor(h[:, :, :], x[:, :, :], mean.unsqueeze(2).broadcast_to(tiles()), ALU.subtract), 1),
                 ("vector", lambda e, _: e.tensor_tensor(h[:, :, :], h[:, :, :], s["rstd"][:, :].unsqueeze(2).broadcast_to(tiles()), ALU.mult), 1),
                 ("scalar", lambda e, _: e.activation(h[:, :, :], h[:, :, :], ACT.Relu), 1)])

        def write_table(view):
            run([("sync", lambda e, _: e.dma_start(table.rearrange("(i p) f -> p i f", p=P), view), 16)])

        def turn(buffer, k):
            def emit(e, _):
                for c in range(BATCH):
                    last = e.transpose(batch_psum(k)[:, c, :], buffer[:, c, :], ident[:, :])
                return last
            return emit

        def dense(inputs, finish):
            steps = [("vector", lambda e, i: inputs[0][0](e, i, stage[0]), 1)]
            if len(inputs) > 1:
                steps.append(("vector", lambda e, i: inputs[1][0](e, i, stage[1]), 1))
            for k in range(len(inputs)):
                steps.append(("tensor", turn(stage[k], k), 1))
            for k, who in zip(range(len(inputs)), ("scalar", "vector")):
                copy = (lambda e, i, k=k: e.copy(turned[k][:, :, :], batch_psum(k))) if who == "scalar" else \
                       (lambda e, i, k=k: e.tensor_copy(turned[k][:, :, :], batch_psum(k)))
                steps.append((who, copy, 1))

            def multiply(e, i):
                for c in range(BATCH):
                    for k, (_, w) in enumerate(inputs):
                        last = e.matmul(batch_psum(2)[:, c, :], lhsT=turned[k][:, c, :], rhs=w[:, :],
                                        start=k == 0, stop=k == len(inputs) - 1)
                return last
            steps.append(("tensor", multiply, 1))
            steps += [(who, (lambda e, i, f=f: f(e, i, batch_psum(2))), 1) for who, f in finish]
            run(steps, BATCHES)

        def from_nodes(view):
            return lambda e, i, out: e.tensor_copy(out[:, :, :], batch(view, i))

        def mean_of_sums(e, i, out):
            return e.tensor_tensor(out[:, :, :], batch(sums, i)[:, :, 0:D],
                                   s["rcount"][:, ds(i * BATCH, BATCH)].unsqueeze(2).broadcast_to(tiles(BATCH)), ALU.mult)

        def plus_row(name, dest):
            return lambda e, i, p: e.tensor_tensor(dest(i), p, row[name][:, :].unsqueeze(1).broadcast_to(tiles(BATCH)), ALU.add)

        def on_every_partition(column, dest):
            def diagonals(e, i):
                return e.tensor_tensor(stage[0][:, :, :], ident[:, :].unsqueeze(1).broadcast_to(tiles(BATCH)),
                                       column[:, ds(i * BATCH, BATCH)].unsqueeze(2).broadcast_to(tiles(BATCH)), ALU.mult)

            def spread(e, i):
                for c in range(BATCH):
                    last = e.matmul(batch_psum(0)[:, c, :], lhsT=ones[:, :], rhs=stage[0][:, c, :], start=True, stop=True)
                return last
            run([("vector", diagonals, 1), ("tensor", spread, 1),
                 ("vector", lambda e, i: e.tensor_copy(batch(dest, i), batch_psum(0)), 1)], BATCHES)

        def edge_pass(name, kind):
            s_idx = sem(name + "_idx")
            s_got = [sem(f"{name}_got{k}") for k in range(SLOTS)]
            s_hot = sem(name + "_hot")
            s_msg = sem(name + "_msg")
            s_pre = sem(name + "_pre")
            s_pe = sem(name + "_pe")
            s_add = sem(name + "_add")
            s_side = [sem(f"{name}_side{k}") for k in range(SLOTS)]
            s_seq = sem(name + "_seq")
            s_exp = sem(name + "_exp")
            s_top = sem(name + "_top")
            width = ATT_ROW if kind in ("max", "weigh") else D
            used = D if kind == "edge" else D + 1
            source = att_table if kind == "max" else table

            def cols(i, k):
                return ds(i * BODY + k * PAIR, PAIR)

            def number(i, k):
                return i * SLOTS + k

            def one_hots(e, i, k):
                e.wait_ge(s_pe, number(i, k) + 1)
                if kind == "first":
                    e.wait_ge(s_idx, number(i, k) + 1)
                e.tensor_tensor(onehot[:, k, :, :], iota[:, :].unsqueeze(1).broadcast_to([P, PAIR, P]),
                                dst_f[:, cols(i, k)].unsqueeze(2).broadcast_to([P, PAIR, P]), ALU.is_equal).then_inc(s_hot, 1)

            with nc.Block() as block:
                @block.gpsimd
                def _(e):
                    def gather(i):
                        for k in range(SLOTS):
                            e.wait_ge(s_idx, number(i, k) + 1)
                            e.wait_ge(s_pe if kind in ("first", "sum") else s_pre, number(i, k) + 1)
                            if kind == "max":
                                e.wait_ge(s_side[k], 16 * i + 16)
                            e.sem_inc(s_gate, 1)
                            for c in range(PAIR):
                                e.indirect_dma_start(ring[:, k, c, 0:width], None, source,
                                                     bass.IndirectOffsetOnAxis(ap=idx[:, k, c:c + 1], axis=0)).then_inc(s_got[k], 16)

                    def hots(i):
                        for k in range(SLOTS):
                            e.wait_ge(s_pe, number(i, k) + 1)
                            e.sem_inc(s_gate, 1)
                            e.tensor_copy(edge_d[:, k, :], dst_f[:, cols(i, k)]).then_inc(s_idx, 1)
                            e.wait_ge(s_idx, number(i, k) + 1)
                            e.sem_inc(s_gate, 1)
                            for c in range(PAIR):
                                last = e.tensor_scalar(onehot[:, k, c, :], iota[:, :], edge_d[:, k, c:c + 1], None, op0=ALU.is_equal)
                            last.then_inc(s_hot, 1)
                    rounds_of(e, ROUNDS, hots if kind == "weigh" else gather)

                if kind != "sum":
                    @block.sync
                    def _(e):
                        def move(i):
                            for k in range(SLOTS):
                                if kind == "max":
                                    e.wait_ge(s_got[k], 16 * PAIR * (i + 1))
                                    e.dma_start(att_rows[:, cols(i, k), :], ring[:, k, :, :]).then_inc(s_side[k], 16)
                                elif kind == "first":
                                    e.wait_ge(s_pre, number(i, k) + 1)
                                    e.dma_start(edge_in[:, k, :, :], bucketed_v[:, cols(i, k), :]).then_inc(s_side[k], 16)
                                elif kind == "edge":
                                    e.wait_ge(s_pre, number(i, k) + 1)
                                    e.dma_start(edge_in[:, k, :, 0:D], bucketed_v[:, cols(i, k), 0:D]).then_inc(s_side[k], 16)
                                else:
                                    e.wait_ge(s_pe, number(i, k) + 1)
                                    e.dma_start(ring[:, k, :, :], att_rows[:, cols(i, k), :]).then_inc(s_got[k], 16 * PAIR)
                        if kind == "max":
                            for k in range(SLOTS):
                                e.sem_inc(s_side[k], 16)
                        rounds_of(e, ROUNDS, move)
                        if kind == "max":
                            for k in range(SLOTS):
                                e.wait_ge(s_side[k], 16 * ROUNDS + 16)

                @block.scalar
                def _(e):
                    if kind in ("first", "max"):
                        e.sem_inc(s_pre, SLOTS)

                    def indices(i, k):
                        e.wait_ge(s_got[k], 16 * PAIR * i)
                        if kind == "first":
                            e.wait_ge(s_side[k], 16 * i + 16)
                            e.copy(dst_f[:, cols(i, k)], edge_in[:, k, :, D + 1])
                            e.copy(src_i[:, cols(i, k)], edge_in[:, k, :, D])
                            e.copy(idx[:, k, :], edge_in[:, k, :, D]).then_inc(s_idx, 1)
                            e.wait_ge(s_idx, number(i, k) + 1)
                            e.sem_inc(s_pre, 1)
                        else:
                            e.copy(idx[:, k, :], src_i[:, cols(i, k)]).then_inc(s_idx, 1)

                    def work(i, k):
                        if kind == "edge":
                            e.wait_ge(s_pre, number(i, k) + 1 + SLOTS)
                            e.activation(extra[:, k, :, :], extra[:, k, :, :], ACT.Relu).then_inc(s_msg, 1)
                        if kind == "max":
                            e.wait_ge(s_got[k], 16 * PAIR * (i + 1))
                            e.wait_ge(s_pe, number(i, k) + 1)
                            for c in range(PAIR):
                                last = e.activation(extra[:, k, c, :], ident[:, :], ACT.Copy, scale=ring[:, k, c, D + 2:D + 3])
                            last.then_inc(s_msg, 1)
                            e.copy(a_src_e[:, cols(i, k)], ring[:, k, :, D + 1]).then_inc(s_pre, 1)
                        if kind == "weigh":
                            e.wait_ge(s_pre, number(i, k) + 1)
                            e.activation(edge_w[:, k, :], edge_w[:, k, :], ACT.Exp).then_inc(s_exp, 1)
                            e.wait_ge(s_exp, number(i, k) + 1)
                            e.wait_ge(s_pe, number(i, k) + 1)
                            for c in range(PAIR):
                                last = e.activation(extra[:, k, c, :], onehot[:, k, c, :], ACT.Copy, scale=edge_w[:, k, c:c + 1])
                            last.then_inc(s_msg, 1)

                    def one(i, more=True):
                        for k in range(SLOTS):
                            work(i, k)
                            if kind != "weigh" and more:
                                indices(i + 1, k)
                    if kind != "weigh":
                        for k in range(SLOTS):
                            indices(0, k)
                    rounds_of(e, ROUNDS - 1, one)
                    one(ROUNDS - 1, False)

                @block.tensor
                def _(e):
                    e.sem_inc(s_pe, SLOTS)

                    def one(i):
                        for k in range(SLOTS):
                            e.wait_ge(s_add, number(i, k) + 1)
                            e.wait_ge(s_hot, number(i, k) + 1)
                            if kind in ("max", "weigh", "edge"):
                                e.wait_ge(s_msg, number(i, k) + 1)
                            if kind != "max":
                                e.wait_ge(s_got[k], 16 * PAIR * (i + 1))
                            for c in range(PAIR):
                                if kind == "max":
                                    last = e.matmul(psum[:, k, c * P:(c + 1) * P], lhsT=onehot[:, k, c, :], rhs=extra[:, k, c, :], start=True, stop=True)
                                else:
                                    lhsT = extra[:, k, c, :] if kind == "weigh" else onehot[:, k, c, :]
                                    rhs = extra[:, k, c, :] if kind == "edge" else ring[:, k, c, 0:used]
                                    last = e.matmul(psum[:, k, 0:used], lhsT=lhsT, rhs=rhs, start=c == 0, stop=c == PAIR - 1)
                            last.then_inc(s_pe, 1)
                    rounds_of(e, ROUNDS, one)

                @block.vector
                def _(e):
                    e.sem_inc(s_add, SLOTS)
                    if kind == "edge":
                        e.sem_inc(s_pre, SLOTS)

                    def at_tile(view, tile, n):
                        return view[:, ds(tile, 1), 0:n].rearrange("p a n -> p (a n)")

                    def look_up(k, rows, tile, to):
                        for c in range(PAIR):
                            last = e.scalar_tensor_tensor(edge_in[:, k, c, 0:P], onehot[:, k, c, :], 1.0, at_tile(rows, tile, P),
                                                          ALU.mult, ALU.mult, accum_out=to[:, c:c + 1])
                        return last

                    def pre(i, k, tile):
                        n = number(i, k)
                        if kind == "edge":
                            e.wait_ge(s_got[k], 16 * PAIR * (i + 1))
                            e.wait_ge(s_side[k], 16 * (i + 1))
                            e.wait_ge(s_pe, n + 1)
                            e.tensor_tensor(extra[:, k, :, :], ring[:, k, :, 0:D], edge_in[:, k, :, 0:D], ALU.add).then_inc(s_pre, 1)
                        if kind == "max":
                            e.wait_ge(s_hot, n + 1)
                            look_up(k, wide, tile, edge_w[:, k, :]).then_inc(s_seq, 1)
                            e.wait_ge(s_seq, n + 1)
                            e.tensor_copy(a_dst_e[:, cols(i, k)], edge_w[:, k, :])
                        if kind == "weigh":
                            e.wait_ge(s_hot, n + 1)
                            look_up(k, wide2, tile, edge_m[:, k, :])
                            e.tensor_tensor(edge_z[:, k, :], a_src_e[:, cols(i, k)], a_dst_e[:, cols(i, k)], ALU.add).then_inc(s_seq, 1)
                            e.wait_ge(s_seq, 2 * n + 1)
                            e.scalar_tensor_tensor(edge_y[:, k, :], edge_z[:, k, :], SLOPE, edge_z[:, k, :], ALU.mult, ALU.max).then_inc(s_seq, 1)
                            e.wait_ge(s_seq, 2 * n + 2)
                            e.wait_ge(s_pe, n + 1)
                            e.tensor_tensor(edge_w[:, k, :], edge_y[:, k, :], edge_m[:, k, :], ALU.subtract).then_inc(s_pre, 1)

                    def add(i, k, tile):
                        n = number(i, k)
                        e.wait_ge(s_pe, n + 1 + SLOTS)
                        if kind == "max":
                            e.tensor_reduce(edge_z[:, k, 0:1], psum[:, k, 0:PAIR * P], axis=AX.X, op=ALU.max).then_inc(s_top, 1)
                            e.wait_ge(s_top, n + 1)
                        e.wait_ge(s_add, n + SLOTS)
                        if kind == "max":
                            to = s["amax"][:, ds(tile, 1)]
                            e.tensor_tensor(to, to, edge_z[:, k, 0:1], ALU.max).then_inc(s_add, 1)
                        else:
                            to = at_tile(sums, tile, used)
                            e.tensor_tensor(to, to, psum[:, k, 0:used], ALU.add).then_inc(s_add, 1)

                    def one(i, more=True):
                        _, tile = nc.values_load_multi_w_load_instructions(
                            tile_i[0:1, ds(i * SLOTS, SLOTS)], engines=(mybir.EngineType.DVE,), min_val=0, max_val=TILES - 1,
                            skip_runtime_bounds_check_because="number of the 49 buckets that start at or before a pair, less one")
                        for k in range(SLOTS + 1):
                            if k < SLOTS:
                                pre(i, k, tile[k])
                            if k > 0:
                                add(i, k - 1, tile[k - 1])
                                if more and kind != "weigh":
                                    one_hots(e, i + 1, k - 1)
                    if kind != "weigh":
                        for k in range(SLOTS):
                            one_hots(e, 0, k)
                    rounds_of(e, ROUNDS - 1, one)
                    one(ROUNDS - 1, False)

        edge_w = sb("edge_w", [P, SLOTS, PAIR])
        edge_z, edge_y, edge_m, edge_d = (sb(n, [P, SLOTS, PAIR]) for n in ("edge_z", "edge_y", "edge_m", "edge_d"))

        def zero_sums():
            run([("vector", lambda e, _: e.memset(sums[:, :, :], 0.0), 1)])

        layer_norm()
        write_table(h[:, :, :])
        zero_sums()
        edge_pass("gin", "first")
        counts = sums[:, :, D]
        run([("vector", lambda e, _: e.tensor_scalar(s["rcount"][:, :], counts, 1.0, None, op0=ALU.max), 1),
             ("vector", lambda e, _: e.reciprocal(s["rcount"][:, :], s["rcount"][:, :]), 1),
             ("vector", lambda e, _: e.tensor_tensor(s["some"][:, :], s["rcount"][:, :], counts, ALU.mult), 1)])
        by_feature = wide[:, :, :].rearrange("p i n -> p (i n)")
        split = BATCH * D // 2

        def mlp_product(w, k):
            def emit(e, i):
                src = turned[0][:, :, :].rearrange("p t n -> p (t n)") if k == 1 else stage[1][:, :, :].rearrange("p t n -> p (t n)")
                for m in range(2):
                    last = e.matmul(psum[:, 2 * k + m, 0:split], lhsT=w[:, :], rhs=src[:, m * split:(m + 1) * split], start=True, stop=True)
                return last
            return emit

        def halves(view):
            return view.rearrange("p (m n) -> p m n", m=2)
        run([
            ("vector", lambda e, i: e.tensor_tensor(stage[0][:, :, :], batch(h, i), batch(sums, i)[:, :, 0:D], ALU.add), 1),
            ("tensor", turn(stage[0], 0), 1),
            ("scalar", lambda e, i: e.copy(turned[0][:, :, :], batch_psum(0)), 1),
            ("tensor", mlp_product(W["L0_gnn_W1"], 1), 1),
            ("scalar", lambda e, i: e.activation(halves(stage[1][:, :, :].rearrange("p t n -> p (t n)")), psum[:, 2:4, 0:split], ACT.Relu,
                                                 bias=col["L0_gnn_b1"][:, :]), 1),
            ("tensor", mlp_product(W["L0_gnn_W2"], 2), 1),
            ("scalar", lambda e, i: e.activation(halves(by_feature[:, ds(i * BATCH * D, BATCH * D)]), psum[:, 4:6, 0:split], ACT.Relu,
                                                 bias=col["L0_gnn_b2"][:, :]), 1),
        ], BATCHES)
        pieces = [(a, min(512, N_NODES - a)) for a in range(0, N_NODES, 512)]

        def column_stats(e, _):
            for k, (a, n) in enumerate(pieces):
                last = e.bn_stats(moments[:, k, :], by_feature[:, a:a + n])
            return last
        scale_c, shift_c = sb("scale_c", [P, 1]), sb("shift_c", [P, 1])
        run([("vector", column_stats, 1),
             ("vector", lambda e, _: e.bn_aggr(mean_var[:, 0, :], moments[:, 0:len(pieces), :].rearrange("p k s -> p (k s)")), 1),
             ("scalar", lambda e, _: e.activation(scale_c[:, :], mean_var[:, 0, 1:2], ACT.Sqrt, bias=eps[:, :]), 1),
             ("vector", lambda e, _: e.reciprocal(scale_c[:, :], scale_c[:, :]), 1),
             ("vector", lambda e, _: e.tensor_tensor(scale_c[:, :], scale_c[:, :], col["L0_gnn_gamma"][:, :], ALU.mult), 1)])
        run([
            ("vector", lambda e, i: e.tensor_scalar(stage[0][:, :, :].rearrange("p t n -> p (t n)"), by_feature[:, ds(i * BATCH * D, BATCH * D)],
                                                    mean_var[:, 0, 0:1], scale_c[:, 0:1], op0=ALU.subtract, op1=ALU.mult), 1),
            ("scalar", lambda e, i: e.activation(stage[1][:, :, :], stage[0][:, :, :], ACT.Identity, bias=col["L0_gnn_beta"][:, :]), 1),
            ("tensor", turn(stage[1], 0), 1),
            ("vector", lambda e, i: e.tensor_tensor(batch(x, i), batch(x, i), batch_psum(0), ALU.add), 1),
        ], BATCHES)

        layer_norm()
        run([("vector", lambda e, _: e.memset(sums[:, :, D + 3:ROW], 0.0), 1)])

        def att(name, to):
            def product(e, i, p):
                return e.tensor_tensor(stage[1][:, :, :], batch(sums, i)[:, :, 0:D], row[name][:, :].unsqueeze(1).broadcast_to(tiles(BATCH)), ALU.mult)

            def total(e, i, p):
                return e.tensor_reduce(s[to][:, ds(i * BATCH, BATCH)], stage[1][:, :, :], axis=AX.X, op=ALU.add)
            return [("vector", product), ("vector", total)]
        dense([(from_nodes(h), W["L1_gnn_W"])],
              [("scalar", lambda e, i, p: e.copy(batch(sums, i)[:, :, 0:D], p))] + att("L1_gnn_att_src", "a_src") + att("L1_gnn_att_dst", "a_dst"))
        least, low = sb("least", [P, 1]), sb("low", [P, 1])
        run([("vector", lambda e, _: e.tensor_reduce(least[:, :], s["a_src"][:, :], axis=AX.X, op=ALU.min), 1),
             ("tensor", lambda e, _: e.transpose(flat[0:1, 0:P], least[:, :], ident[:, :]), 1),
             ("vector", lambda e, _: e.tensor_reduce(junk[0:1, 0:1], flat[0:1, 0:P], axis=AX.X, op=ALU.min), 1),
             ("tensor", lambda e, _: e.matmul(flat[:, 512:513], lhsT=ones[0:1, :], rhs=junk[0:1, 0:1], start=True, stop=True), 1),
             ("vector", lambda e, _: e.tensor_copy(low[:, :], flat[:, 512:513]), 1),
             ("vector", lambda e, _: e.memset(sums[:, :, D:D + 1], 1.0), 1),
             ("vector", lambda e, _: e.tensor_copy(sums[:, :, D + 1], s["a_src"][:, :]), 1),
             ("vector", lambda e, _: e.tensor_scalar(sums[:, :, D + 2], s["a_src"][:, :], low[:, 0:1], None, op0=ALU.subtract), 1),
             ("sync", lambda e, _: e.dma_start(att_table.rearrange("(i p) w -> p i w", p=P), sums[:, :, :]), 16),
             ("vector", lambda e, _: e.memset(s["amax"][:, :], 0.0), 1)])
        on_every_partition(s["a_dst"], wide)
        edge_pass("att_max", "max")
        run([("vector", lambda e, _: e.scalar_tensor_tensor(s["top"][:, :], s["amax"][:, :], low[:, 0:1], s["a_dst"][:, :], ALU.add, ALU.add), 1),
             ("vector", lambda e, _: e.scalar_tensor_tensor(s["mean"][:, :], s["top"][:, :], SLOPE, s["top"][:, :], ALU.mult, ALU.max), 1)])
        on_every_partition(s["mean"], wide2)
        zero_sums()
        edge_pass("att_sum", "weigh")
        run([("vector", lambda e, _: e.tensor_scalar(s["rden"][:, :], sums[:, :, D], 1e-16, None, op0=ALU.add), 1),
             ("vector", lambda e, _: e.reciprocal(s["rden"][:, :], s["rden"][:, :]), 1),
             ("vector", lambda e, _: e.tensor_tensor(h[:, :, :], sums[:, :, 0:D], s["rden"][:, :].unsqueeze(2).broadcast_to(tiles()), ALU.mult), 1),
             ("vector", lambda e, _: e.tensor_tensor(h[:, :, :], h[:, :, :], row["L1_gnn_bias"][:, :].unsqueeze(1).broadcast_to(tiles()), ALU.add), 1),
             ("vector", lambda e, _: e.scalar_tensor_tensor(x[:, :, :].rearrange("p i f -> p (i f)"), h[:, :, :].rearrange("p i f -> p (i f)"), 0.0,
                                                            x[:, :, :].rearrange("p i f -> p (i f)"), ALU.max, ALU.add), 1)])

        layer_norm()
        for n in (1, 2, 3):
            write_table(h[:, :, :])
            zero_sums()
            edge_pass(f"sage{n}", "sum")
            finish = [("vector", plus_row(f"L2_gnn_b{n}", lambda i: batch(h, i)))]
            if n == 1:
                finish.append(("scalar", lambda e, i, p: e.activation(batch(h, i), batch(h, i), ACT.Relu)))
            if n == 3:
                finish.append(("vector", lambda e, i, p: e.tensor_tensor(batch(x, i), batch(x, i), batch(h, i), ALU.add)))
            dense([(mean_of_sums, W[f"L2_gnn_Wl{n}"]), (from_nodes(h), W[f"L2_gnn_Wr{n}"])], finish)

        layer_norm()
        dense([(from_nodes(h), W["node"])], [("vector", plus_row("L3_gnn_b1a", lambda i: batch(wide, i)))])
        write_table(wide[:, :, :])
        zero_sums()
        edge_pass("meta", "edge")
        dense([(mean_of_sums, W["L3_gnn_W1b"])],
              [("vector", lambda e, i, p: e.tensor_tensor(stage[1][:, :, :], row["L3_gnn_b1b"][:, :].unsqueeze(1).broadcast_to(tiles(BATCH)),
                                                          s["some"][:, ds(i * BATCH, BATCH)].unsqueeze(2).broadcast_to(tiles(BATCH)), ALU.mult)),
               ("vector", lambda e, i, p: e.tensor_tensor(batch(wide, i), stage[1][:, :, :], p, ALU.add))])
        run([("vector", lambda e, _: e.tensor_copy(junk[0:D_EDGE, :], u0[:, :].broadcast_to([D_EDGE, P])), 1),
             ("tensor", lambda e, _: e.matmul(flat[:, 0:D], lhsT=junk[0:D_EDGE, :], rhs=W["u"][:, :], start=True, stop=True), 1),
             ("vector", lambda e, _: e.tensor_tensor(row["L3_gnn_b2a"][:, :], row["L3_gnn_b2a"][:, :], flat[:, 0:D], ALU.add), 1)])
        dense([(from_nodes(h), W["h"]), (from_nodes(wide), W["agg"])],
              [("vector", plus_row("L3_gnn_b2a", lambda i: batch(wide2, i))),
               ("scalar", lambda e, i, p: e.activation(batch(wide2, i), batch(wide2, i), ACT.Relu))])
        dense([(from_nodes(wide2), W["L3_gnn_W2b"])],
              [("vector", plus_row("L3_gnn_b2b", lambda i: batch(wide2, i))),
               ("vector", lambda e, i, p: e.tensor_tensor(batch(x, i), batch(x, i), batch(wide2, i), ALU.add))])
        s_out = sem("s_out")

        def store(e, _):
            e.dma_start(out[0:full_nodes * P, :].rearrange("(i p) f -> p i f", p=P), x[:, 0:full_nodes, :]).then_inc(s_out, 16)
            e.dma_start(out[full_nodes * P:N_NODES, :], x[0:N_NODES - full_nodes * P, full_nodes, :]).then_inc(s_out, 16)
            e.wait_ge(s_out, 32)
            return e.nop()
        run([("sync", store, 1)])


def kernel(**inputs):
    import numpy as np
    import concourse.bacc as bacc
    from concourse.bass_utils import run_bass_kernel_spmd as launch

    a = {k: np.ascontiguousarray(v) for k, v in inputs.items()}
    for n in (1, 2, 3):
        for side in "lr":
            a[f"L2_gnn_W{side}{n}"] = np.ascontiguousarray(a[f"L2_gnn_W{side}{n}"].T)
    for name in ("src", "dst"):
        v = a.pop(name)
        a[name + "_full"] = np.ascontiguousarray(v[:FULL_IN * P].reshape(FULL_IN, P).T)
        a[name + "_tail"] = np.ascontiguousarray(v[FULL_IN * P:].reshape(TAIL_IN, 1))
    a["attr_t"] = np.ascontiguousarray(a.pop("edge_attr_64").T)
    nc = bacc.Bacc("TRN2", target_bir_lowering=False, num_devices=1)
    t = {k: nc.dram_tensor("in_" + k, v.shape, mybir.dt.from_np(v.dtype), kind="ExternalInput").ap() for k, v in a.items()}
    out = nc.dram_tensor("out", (N_NODES, D), fp32, kind="ExternalOutput").ap()
    build(nc, t, out)
    r = launch(nc, [{"in_" + k: v for k, v in a.items()}], core_ids=[0])
    return r.results[0]["out"]
```

```python
import concourse.bass as bass
from concourse import mybir
from contextlib import ExitStack

P = 128
N_NODES, N_EDGES, D, D_EDGE = 6250, 200000, 128, 64
TILES = -(-N_NODES // P)
NODES = TILES * P
PAIR, SLOTS = 2, 4
BODY = PAIR * SLOTS
FULL_IN = N_EDGES // P
TAIL_IN = N_EDGES - FULL_IN * P
COLS_IN = FULL_IN + (TAIL_IN > 0)
PAIRS = -(-(N_EDGES // (PAIR * P) + TILES) // SLOTS) * SLOTS
CHUNKS = PAIRS * PAIR
PAIR_COLS = -(-PAIRS // P)
ROUNDS = CHUNKS // BODY
EDGE_ROW = D + 2
ATT_ROW = D + 4
ROW = D + 4
BATCH = 7
BATCHES = TILES // BATCH
assert BATCH * BATCHES == TILES
EPS = 1e-5
SLOPE = 0.2

fp32, i32 = mybir.dt.float32, mybir.dt.int32
ALU = mybir.AluOpType
ACT = mybir.ActivationFunctionType
AX = mybir.AxisListType
ds = bass.ds


class Baton:

    def __init__(self, sem):
        self.sem, self.at = sem, 0


def relay(nc, baton, steps, rounds=1):
    start, length = baton.at, sum(inc for _, _, inc in steps)

    def program(name):
        def build(eng):
            def one_round(i):
                before = start
                for who, emit, inc in steps:
                    if who == name:
                        eng.wait_ge(baton.sem, i * length + before)
                        emit(eng, i).then_inc(baton.sem, inc)
                    before += inc
            if rounds == 1:
                one_round(0)
            else:
                with eng.Fori(0, rounds) as i:
                    one_round(i)
        return build

    with nc.Block() as block:
        on = {"sync": block.sync, "gpsimd": block.gpsimd, "vector": block.vector,
              "scalar": block.scalar, "tensor": block.tensor}
        for name in on:
            if any(who == name for who, _, _ in steps):
                on[name](program(name))
    baton.at = start + rounds * length


def rounds_of(eng, n, body, first=0, last=0):
    for i in range(first):
        body(i)
    with eng.Fori(first, n - last) as i:
        body(i)
    for i in range(n - last, n):
        body(i)


def build(nc, t, out):
    ctx = ExitStack()
    with ctx:
        def sb(name, shape, dt=fp32):
            return ctx.enter_context(nc.sbuf_tensor(name, shape, dt))

        def sem(name):
            return ctx.enter_context(nc.semaphore(name))

        def dram(name, shape, dt=fp32):
            return nc.dram_tensor(name, shape, dt, kind="Internal").ap()

        table = dram("table", (NODES, D))
        att_table = dram("att_table", (NODES, ATT_ROW))
        bucketed = dram("bucketed", (P * CHUNKS, EDGE_ROW))
        att_rows = dram("att_rows", (P, CHUNKS, ATT_ROW))
        pair_tiles = dram("pair_tiles", (P, PAIR_COLS), i32)
        bucketed_v = bucketed.rearrange("(p c) w -> p c w", p=P)

        x = sb("x", [P, TILES, D])
        h = sb("h", [P, TILES, D])
        sums = sb("sums", [P, TILES, ROW])
        wide = sb("wide", [P, TILES, D])
        wide2 = sb("wide2", [P, TILES, D])
        src_i = sb("src_i", [P, CHUNKS], i32)
        dst_f = sb("dst_f", [P, CHUNKS])
        tile_i = sb("tile_i", [1, PAIRS + SLOTS], i32)
        a_src_e = sb("a_src_e", [P, CHUNKS])
        a_dst_e = sb("a_dst_e", [P, CHUNKS])
        ring = sb("ring", [P, SLOTS, PAIR, ROW])
        onehot = sb("onehot", [P, SLOTS, PAIR, P])
        extra = sb("extra", [P, SLOTS, PAIR, P])
        edge_in = sb("edge_in", [P, SLOTS, PAIR, EDGE_ROW])
        idx = sb("idx", [P, SLOTS, PAIR], i32)
        junk = sb("junk", [P, P])
        stage = [sb(f"stage{k}", [P, BATCH, D]) for k in range(2)]
        turned = [sb(f"turned{k}", [P, BATCH, D]) for k in range(2)]
        ident = sb("ident", [P, P])
        ones = sb("ones", [P, P])
        before = sb("before", [P, P])
        iota = sb("iota", [P, P])
        eps = sb("eps", [P, 1])
        psum = ctx.enter_context(nc.psum_tensor("psum", [P, 8, 512], fp32))
        flat = psum[:, :, :].rearrange("p b n -> p (b n)")

        def batch_psum(k):
            return flat[:, 1024 * k:1024 * k + BATCH * D].rearrange("p (t n) -> p t n", t=BATCH)

        def pair_psum(k):
            return psum[:, k, :].rearrange("p (c n) -> p c n", c=PAIR)

        relay_baton = Baton(sem("relay"))
        moves = {name: Baton(sem("nodes_" + name)) for name in ("vector", "scalar", "staged", "turned", "copied", "product", "finished")}
        s_gate = sem("s_gate")

        def run(steps, rounds=1):
            relay(nc, relay_baton, steps, rounds)

        def batch(view, i):
            return view[:, ds(i * BATCH, BATCH), :]

        W = {}
        loads = []
        for name in ("L0_gnn_W1", "L0_gnn_W2", "L1_gnn_W", "L2_gnn_Wl1", "L2_gnn_Wr1", "L2_gnn_Wl2", "L2_gnn_Wr2",
                     "L2_gnn_Wl3", "L2_gnn_Wr3", "L3_gnn_W1b", "L3_gnn_W2b"):
            W[name] = sb("w_" + name, [P, D])
            loads.append((W[name][:, :], t[name]))
        W["edge"] = sb("w_edge", [D_EDGE, D])
        W["u"] = sb("w_u", [D_EDGE, D])
        for name in ("node", "h", "agg"):
            W[name] = sb("w_" + name, [P, D])
        loads += [(W["node"][:, :], t["L3_gnn_W1a"][0:D, :]), (W["edge"][:, :], t["L3_gnn_W1a"][D:D + D_EDGE, :]),
                  (W["h"][:, :], t["L3_gnn_W2a"][0:D, :]), (W["agg"][:, :], t["L3_gnn_W2a"][D:2 * D, :]),
                  (W["u"][:, :], t["L3_gnn_W2a"][2 * D:2 * D + D_EDGE, :])]
        col = {}
        for name in ("L0_gnn_b1", "L0_gnn_b2", "L0_gnn_gamma", "L0_gnn_beta"):
            col[name] = sb("c_" + name, [P, 1])
            loads.append((col[name][:, :], t[name].rearrange("(f a) -> f a", a=1)))
        u0 = sb("u0", [D_EDGE, 1])
        loads.append((u0[:, :], t["L3_gnn_u"][0, :].rearrange("(f a) -> f a", a=1)))
        row = {}
        for name in ("L1_gnn_att_src", "L1_gnn_att_dst", "L1_gnn_bias", "L2_gnn_b1", "L2_gnn_b2", "L2_gnn_b3",
                     "L3_gnn_b1a", "L3_gnn_b1b", "L3_gnn_b2a", "L3_gnn_b2b"):
            row[name] = sb("r_" + name, [P, D])
            loads.append((row[name][:, :], t[name].partition_broadcast(P)))
        full_nodes = N_NODES // P
        loads += [(x[:, 0:full_nodes, :], t["x"][0:full_nodes * P, :].rearrange("(i p) f -> p i f", p=P)),
                  (x[0:N_NODES - full_nodes * P, full_nodes, :], t["x"][full_nodes * P:N_NODES, :])]

        def load_all(eng, _):
            for dst, src in loads[:-1]:
                eng.dma_start(dst, src).then_inc(s_load, 16)
            return eng.dma_start(*loads[-1])

        def part(tensor, at, n):
            whole = tensor[:, :, :].rearrange("p i w -> p (i w)")
            return whole[:, at:at + n]

        meta = part(h, 0, 2 * COLS_IN).rearrange("p (c w) -> p c w", w=2)
        slot_i = part(h, 3136, COLS_IN).bitcast(i32)
        tile_in = part(h, 4704, COLS_IN)
        tile_of, pair_no = sb("tile_of", [P, PAIR_COLS]), sb("pair_no", [P, PAIR_COLS])
        tile_of_i = sb("tile_of_i", [P, PAIR_COLS], i32)
        dst_in = part(wide, 4096, COLS_IN).bitcast(i32)
        empty = part(wide2, 0, 16 * EDGE_ROW).rearrange("p (c w) -> p c w", c=16)
        src_in = part(wide2, 2112, COLS_IN).bitcast(i32)
        attr = part(wide2, 3712, BODY * P)[0:D_EDGE, :].rearrange("p (k n) -> p k n", k=SLOTS)
        mask = part(sums, 0, COLS_IN).bitcast(i32)
        scan = part(sums, 2048, COLS_IN)
        slot = part(sums, 4096, COLS_IN)
        small = {n: sb("s_" + n, [P, TILES]) for n in
                 ("bucket", "partial", "count", "chunks", "ends", "start", "rcount", "some", "a_src", "a_dst",
                  "amax", "top", "mean", "rstd", "rden")}
        small_i = sb("small_i", [P, TILES], i32)
        moments = sb("moments", [P, TILES, 6])
        mean_var = sb("mean_var", [P, TILES, 2])

        s_load, s_edges, s_empty = sem("s_load"), sem("s_edges"), sem("s_empty")
        n_loads = len(loads)

        def consts_pool(e, _):
            e.memset(ident[:, :], 0.0)
            e.memset(before[:, :], 1.0)
            e.memset(dst_in, NODES)
            e.memset(src_in, 0)
            e.memset(empty, 0.0)
            e.memset(slot, 1.0)
            e.memset(ring[:, :, :, :], 0.0)
            e.memset(x[:, :, :], 0.0)
            e.iota(iota[:, :], [[1, P]], base=0, channel_multiplier=0, allow_small_or_imprecise_dtypes=True)
            e.iota(small["bucket"][:, :], [[1, TILES]], base=0, channel_multiplier=0,
                   allow_small_or_imprecise_dtypes=True)
            e.iota(pair_no[:, :], [[1, PAIR_COLS]], base=0, channel_multiplier=PAIR_COLS, allow_small_or_imprecise_dtypes=True)
            e.memset(ones[:, :], 1.0)
            e.memset(tile_of[:, :], -1.0)
            return e.memset(eps[:, :], EPS)

        def consts_pool2(e, _):
            e.affine_select(out=ident[:, :], in_=ident[:, :], compare_op=ALU.not_equal, fill=1.0, base=0,
                            pattern=[[-1, P]], channel_multiplier=1)
            e.affine_select(out=before[:, :], in_=before[:, :], compare_op=ALU.is_gt, fill=0.0, base=0,
                            pattern=[[1, P]], channel_multiplier=-1)
            e.memset(empty[:, :, D + 1:D + 2], -1.0)
            return e.memset(ring[:, :, :, D:D + 1], 1.0)

        def load_edges(e, _):
            e.dma_start(dst_in[:, 0:FULL_IN], t["dst_full"]).then_inc(s_edges, 16)
            e.dma_start(dst_in[0:TAIL_IN, FULL_IN:COLS_IN], t["dst_tail"]).then_inc(s_edges, 16)
            e.dma_start(src_in[:, 0:FULL_IN], t["src_full"]).then_inc(s_edges, 16)
            e.dma_start(src_in[0:TAIL_IN, FULL_IN:COLS_IN], t["src_tail"]).then_inc(s_edges, 16)
            return load_all(e, _)

        def fill_empty(e, _):
            e.dma_start(bucketed_v.rearrange("p (r c) w -> p r (c w)", c=16),
                        empty.rearrange("p c w -> p (c w)").unsqueeze(1).broadcast_to([P, CHUNKS // 16, 16 * EDGE_ROW])
                        ).then_inc(s_empty, 16)
            return e.nop()

        def split_dst(e, _):
            e.wait_ge(s_edges, 64)
            e.wait_ge(s_load, 16 * (n_loads - 1))
            e.tensor_single_scalar(mask, dst_in, 7, op=ALU.arith_shift_right)
            return e.tensor_single_scalar(slot_i, dst_in, P - 1, op=ALU.bitwise_and)

        def to_float(e, _):
            e.tensor_copy(tile_in, mask)
            e.tensor_copy(meta[:, :, 0], src_in)
            return e.tensor_copy(meta[:, :, 1], slot_i)

        run([("gpsimd", consts_pool, 1), ("gpsimd", consts_pool2, 1), ("sync", load_edges, 16),
             ("sync", fill_empty, 1), ("vector", split_dst, 1), ("vector", to_float, 1)])

        def count_bucket(e, i):
            return e.scalar_tensor_tensor(scan, tile_in, small["bucket"][:, ds(i, 1)], slot, ALU.is_equal, ALU.mult,
                                          accum_out=small["partial"][:, ds(i, 1)])

        run([("vector", count_bucket, 1)], TILES)

        s = small
        run([
            ("tensor", lambda e, _: e.matmul(flat[:, 0:TILES], lhsT=before[:, :], rhs=s["partial"][:, :], start=True, stop=True), 1),
            ("tensor", lambda e, _: e.matmul(flat[:, 512:512 + TILES], lhsT=ones[:, :], rhs=s["partial"][:, :], start=True, stop=True), 1),
            ("vector", lambda e, _: e.tensor_scalar(small_i[:, :], flat[:, 512:512 + TILES], float(PAIR * P - 1), None, op0=ALU.add), 1),
            ("vector", lambda e, _: e.tensor_single_scalar(small_i[:, :], small_i[:, :], 8, op=ALU.arith_shift_right), 1),
            ("vector", lambda e, _: e.tensor_copy(s["chunks"][:, :], small_i[:, :]), 1),
            ("vector", lambda e, _: e.tensor_tensor_scan(s["ends"][:, :], ones[:, 0:TILES], s["chunks"][:, :], 0.0, ALU.mult, ALU.add), 1),
            ("vector", lambda e, _: e.tensor_tensor(s["ends"][:, :], s["ends"][:, :], s["chunks"][:, :], ALU.subtract), 1),
            ("vector", lambda e, _: e.scalar_tensor_tensor(s["start"][:, :], s["ends"][:, :], float(PAIR * P), flat[:, 0:TILES], ALU.mult, ALU.add), 1),
        ])

        s_mask, s_scan, s_place = sem("s_mask"), sem("s_scan"), sem("s_place")
        masks = [mask, part(wide, 0, COLS_IN).bitcast(i32)]
        scans = [scan, part(wide, 2048, COLS_IN)]
        with nc.Block() as block:
            @block.vector
            def _(e):
                e.sem_inc(s_place, 2)

                def is_in_bucket(i, k):
                    e.wait_ge(s_place, i + 1)
                    e.tensor_scalar(masks[k], tile_in, small["bucket"][:, ds(i, 1)], None, op0=ALU.is_equal).then_inc(s_mask, 1)

                def bucket(i, k, more=True):
                    e.wait_ge(s_mask, i + 1)
                    e.tensor_tensor_scan(scans[k], masks[k], masks[k], s["start"][:, ds(i, 1)], ALU.add, ALU.max).then_inc(s_scan, 1)
                    e.scalar_tensor_tensor(tile_of[:, :], pair_no[:, :], s["ends"][:, ds(i, 1)], tile_of[:, :], ALU.is_ge, ALU.add)
                    if more:
                        is_in_bucket(i + 1, 1 - k)
                    e.wait_ge(s_scan, i + 1)
                    e.sem_inc(s_gate, 1)
                    e.copy_predicated(slot, masks[k], scans[k]).then_inc(s_place, 1)
                is_in_bucket(0, 0)
                with e.Fori(0, TILES // 2) as i:
                    for k in range(2):
                        bucket(2 * i + k, k)
                bucket(TILES - 1, 0, more=False)
        assert TILES % 2 == 1

        def all_placed(e, _):
            e.wait_ge(s_place, TILES + 2)
            return e.nop()
        run([("vector", all_placed, 1)])

        run([
            ("vector", lambda e, _: e.tensor_copy(tile_of_i[:, :], tile_of[:, :]), 1),
            ("sync", lambda e, _: e.dma_start(pair_tiles, tile_of_i[:, :]), 16),
            ("sync", lambda e, _: e.dma_start(tile_i[:, :], pair_tiles.rearrange("p j -> (p j)")[0:PAIRS + SLOTS].unsqueeze(0)), 16),
            ("vector", lambda e, _: e.tensor_scalar(mask, slot, -1.0, None, op0=ALU.add), 1),
            ("vector", lambda e, _: e.tensor_single_scalar(slot_i, mask, P - 1, op=ALU.bitwise_and), 1),
            ("vector", lambda e, _: e.tensor_single_scalar(mask, mask, 7, op=ALU.arith_shift_right), 1),
            ("vector", lambda e, _: e.scalar_tensor_tensor(slot_i, slot_i, float(CHUNKS), mask, ALU.mult, ALU.add), 1),
        ])

        def scatter_edges():
            in_rounds = FULL_IN // BODY
            s_attr = [sem(f"s_attr{k}") for k in range(SLOTS)]
            s_mul = sem("s_mul")
            s_row = sem("s_row")
            s_meta = sem("s_meta")
            s_sent = [sem(f"s_sent{k}") for k in range(SLOTS)]
            rest = FULL_IN - in_rounds * BODY

            def cols(i, k):
                return ds(i * BODY + k * PAIR, PAIR)

            with nc.Block() as block:
                @block.sync
                def _(e):
                    def one(i):
                        for k in range(SLOTS):
                            e.wait_ge(s_mul, SLOTS * i + k + 1)
                            e.dma_start(attr[:, k, :], t["attr_t"][:, ds((i * BODY + k * PAIR) * P, PAIR * P)]).then_inc(s_attr[k], 16)
                    rounds_of(e, in_rounds, one)

                @block.tensor
                def _(e):
                    e.sem_inc(s_mul, SLOTS)
                    def one(i):
                        for k in range(SLOTS):
                            e.wait_ge(s_attr[k], 16 * i + 16)
                            e.wait_ge(s_row, SLOTS * i + k + 1)
                            for c in range(PAIR):
                                last = e.matmul(pair_psum(k)[:, c, 0:D], lhsT=attr[:, k, c * P:(c + 1) * P],
                                                rhs=W["edge"][:, :], start=True, stop=True)
                            last.then_inc(s_mul, 1)
                    rounds_of(e, in_rounds, one)

                @block.scalar
                def _(e):
                    e.sem_inc(s_row, SLOTS)
                    def one(i):
                        for k in range(SLOTS):
                            e.wait_ge(s_sent[k], 16 * PAIR * i)
                            e.wait_ge(s_mul, SLOTS * i + k + 1 + SLOTS)
                            e.copy(idx[:, k, :], slot_i[:, cols(i, k)])
                            e.copy(ring[:, k, :, 0:D], pair_psum(k)[:, :, 0:D]).then_inc(s_row, 1)
                    rounds_of(e, in_rounds, one, first=1)

                @block.vector
                def _(e):
                    def one(i):
                        for k in range(SLOTS):
                            e.wait_ge(s_sent[k], 16 * PAIR * i)
                            e.tensor_copy(ring[:, k, :, D:D + 2], meta[:, cols(i, k), :]).then_inc(s_meta, 1)
                    rounds_of(e, in_rounds, one, first=1)

                @block.gpsimd
                def _(e):
                    e.wait_ge(s_empty, 16)
                    def one(i):
                        for k in range(SLOTS):
                            e.wait_ge(s_row, SLOTS * i + k + 1 + SLOTS)
                            e.wait_ge(s_meta, SLOTS * i + k + 1)
                            e.sem_inc(s_gate, 1)
                            for c in range(PAIR):
                                e.indirect_dma_start(bucketed, bass.IndirectOffsetOnAxis(ap=idx[:, k, c:c + 1], axis=0),
                                                     ring[:, k, c, 0:EDGE_ROW], None).then_inc(s_sent[k], 16)
                    rounds_of(e, in_rounds, one)
                    for k in range(SLOTS):
                        e.wait_ge(s_sent[k], 16 * PAIR * in_rounds)

            left = rest + (TAIL_IN > 0)
            sizes = [P] * rest + [TAIL_IN] * (TAIL_IN > 0)
            first = in_rounds * BODY
            n_left = N_EDGES - first * P
            s_left = sem("s_left")
            places = [(c // PAIR, c % PAIR, n) for c, n in enumerate(sizes)]

            def send(e, _):
                for k, c, n in places:
                    e.indirect_dma_start(bucketed, bass.IndirectOffsetOnAxis(ap=idx[0:n, k, c:c + 1], axis=0),
                                         ring[0:n, k, c, 0:EDGE_ROW], None).then_inc(s_left, 16)
                e.wait_ge(s_left, 16 * left)
                return e.nop()

            def multiply(e, _):
                for k, c, n in places:
                    last = e.matmul(pair_psum(k)[0:n, c, 0:D], lhsT=attr[:, k, c * P:c * P + n], rhs=W["edge"][:, :], start=True, stop=True)
                return last

            def copy_terms(e, _):
                for k, c, n in places:
                    last = e.copy(ring[0:n, k, c, 0:D], pair_psum(k)[0:n, c, 0:D])
                return last

            def copy_meta(e, _):
                for j, (k, c, _n) in enumerate(places):
                    e.tensor_copy(idx[:, k, c:c + 1], slot_i[:, first + j:first + j + 1])
                    last = e.tensor_copy(ring[:, k, c, D:D + 2], meta[:, first + j, :])
                return last

            run([("sync", lambda e, _: e.dma_start(part(wide2, 3712, n_left)[0:D_EDGE, :], t["attr_t"][:, first * P:N_EDGES]), 16),
                 ("tensor", multiply, 1), ("scalar", copy_terms, 1), ("vector", copy_meta, 1), ("gpsimd", send, 1),
                 ("gpsimd", lambda e, _: e.memset(ring[:, :, :, D:D + 1], 1.0), 1)])

        scatter_edges()

        def tiles(n=TILES):
            return [P, n, D]

        def layer_norm(store):
            def stats(e, i):
                for k in range(BATCH):
                    last = e.bn_stats(moments[:, ds(i * BATCH + k, 1), :].rearrange("p a s -> p (a s)"),
                                      x[:, ds(i * BATCH + k, 1), :].rearrange("p a f -> p (a f)"))
                return last
            run([("vector", stats, 1)], BATCHES)

            def aggregate(e, _):
                for k in range(TILES):
                    last = e.bn_aggr(mean_var[:, k, :], moments[:, k, :])
                return last
            mean, var = mean_var[:, :, 0], mean_var[:, :, 1]
            run([("vector", aggregate, 1),
                 ("scalar", lambda e, _: e.activation(s["rstd"][:, :], var, ACT.Sqrt, bias=eps[:, :]), 1),
                 ("vector", lambda e, _: e.reciprocal(s["rstd"][:, :], s["rstd"][:, :]), 1),
                 ("vector", lambda e, _: e.tensor_copy(s["mean"][:, :], mean), 1)])
            done, rectified = moves["vector"], moves["scalar"]

            with nc.Block() as block:
                @block.vector
                def _(e):
                    def normalise(i):
                        for k in range(BATCH):
                            t = ds(i * BATCH + k, 1)
                            last = e.tensor_scalar(h[:, t, :].rearrange("p a f -> p (a f)"), x[:, t, :].rearrange("p a f -> p (a f)"),
                                                   s["mean"][:, t], s["rstd"][:, t], op0=ALU.subtract, op1=ALU.mult)
                        last.then_inc(done.sem, 1)
                    rounds_of(e, BATCHES, normalise)

                @block.scalar
                def _(e):
                    def rectify(i):
                        e.wait_ge(done.sem, done.at + i + 1)
                        e.activation(batch(h, i), batch(h, i), ACT.Relu).then_inc(rectified.sem, 1)
                    rounds_of(e, BATCHES, rectify)
                if store:
                    @block.sync
                    def _(e):
                        def write(i):
                            e.wait_ge(rectified.sem, rectified.at + i + 1)
                            e.dma_start(batch(table_nodes, i), batch(h, i)).then_inc(stored.sem, 16)
                        rounds_of(e, BATCHES, write)
            done.at += BATCHES
            rectified.at += BATCHES
            stored.at += 16 * BATCHES * store

        table_nodes = table.rearrange("(i p) f -> p i f", p=P)
        stored = Baton(sem("s_stored"))

        def turn(buffer, k):
            def emit(e, _):
                for c in range(BATCH):
                    last = e.transpose(batch_psum(k)[:, c, :], buffer[:, c, :], ident[:, :])
                return last
            return emit

        def dense(inputs, finish, reader=0, store=None):
            n_in, n_fin = len(inputs), len(finish)
            staged, turned_, copied, product, finished = (moves[n] for n in ("staged", "turned", "copied", "product", "finished"))

            def program_of(name):
                def program(e):
                    def fill(i):
                        for k, (who, emit, _) in enumerate(inputs):
                            if who == name:
                                emit(e, i, stage[k]).then_inc(staged.sem, 1)

                    def one(i, more=True):
                        for k, (who, _, _) in enumerate(inputs):
                            if who == name:
                                e.wait_ge(turned_.sem, turned_.at + i + 1)
                                (e.copy if who == "scalar" else e.tensor_copy)(
                                    turned[k][:, :, :], batch_psum(k)).then_inc(copied.sem, 1)
                        if more:
                            fill(i + 1)
                        for k, (who, emit) in enumerate(finish):
                            if who == name:
                                e.wait_ge(product.sem, product.at + i + 1)
                                e.wait_ge(finished.sem, finished.at + n_fin * (i + 1) + k)
                                emit(e, i, batch_psum(2)).then_inc(finished.sem, 1)
                    fill(0)
                    rounds_of(e, BATCHES - 1, one)
                    one(BATCHES - 1, False)
                return program

            with nc.Block() as block:
                @block.tensor
                def _(e):
                    e.sem_inc(finished.sem, n_fin)

                    def one(i):
                        e.wait_ge(staged.sem, staged.at + n_in * (i + 1))
                        for k in range(n_in):
                            last = turn(stage[k], k)(e, i)
                        last.then_inc(turned_.sem, 1)
                        e.wait_ge(copied.sem, copied.at + n_in * (i + 1))
                        e.wait_ge(finished.sem, finished.at + n_fin * i + reader + 1)
                        for c in range(BATCH):
                            for k, (_, _, w) in enumerate(inputs):
                                last = e.matmul(batch_psum(2)[:, c, :], lhsT=turned[k][:, c, :], rhs=w[:, :],
                                                start=k == 0, stop=k == n_in - 1)
                        last.then_inc(product.sem, 1)
                    rounds_of(e, BATCHES, one)

                block.scalar(program_of("scalar"))
                block.vector(program_of("vector"))
                if store is not None:
                    @block.sync
                    def _(e):
                        def write(i):
                            e.wait_ge(finished.sem, finished.at + n_fin * (i + 2))
                            e.dma_start(batch(table_nodes, i), batch(store, i)).then_inc(stored.sem, 16)
                        rounds_of(e, BATCHES, write)
                    stored.at += 16 * BATCHES
            staged.at += n_in * BATCHES
            turned_.at += BATCHES
            copied.at += n_in * BATCHES
            product.at += BATCHES
            finished.at += n_fin * (BATCHES + 1)

        def nodes_of(view):
            return "scalar", lambda e, i, out: e.copy(out[:, :, :], batch(view, i))

        def mean_of_sums():
            return "vector", lambda e, i, out: e.tensor_tensor(
                out[:, :, :], batch(sums, i)[:, :, 0:D], s["rcount"][:, ds(i * BATCH, BATCH)].unsqueeze(2).broadcast_to(tiles(BATCH)), ALU.mult)

        def plus_row(name, dest):
            return lambda e, i, p: e.tensor_tensor(dest(i), p, row[name][:, :].unsqueeze(1).broadcast_to(tiles(BATCH)), ALU.add)

        def on_every_partition(column, dest):
            def diagonals(e, i):
                return e.tensor_tensor(stage[0][:, :, :], ident[:, :].unsqueeze(1).broadcast_to(tiles(BATCH)),
                                       column[:, ds(i * BATCH, BATCH)].unsqueeze(2).broadcast_to(tiles(BATCH)), ALU.mult)

            def spread(e, i):
                for c in range(BATCH):
                    last = e.matmul(batch_psum(0)[:, c, :], lhsT=ones[:, :], rhs=stage[0][:, c, :], start=True, stop=True)
                return last
            run([("vector", diagonals, 1), ("tensor", spread, 1),
                 ("vector", lambda e, i: e.tensor_copy(batch(dest, i), batch_psum(0)), 1)], BATCHES)

        def edge_pass(name, kind):
            s_idx = sem(name + "_idx")
            s_got = [sem(f"{name}_got{k}") for k in range(SLOTS)]
            s_hot = sem(name + "_hot")
            s_msg = sem(name + "_msg")
            s_pre = sem(name + "_pre")
            s_pe = sem(name + "_pe")
            s_add = sem(name + "_add")
            s_side = [sem(f"{name}_side{k}") for k in range(SLOTS)]
            s_seq = sem(name + "_seq")
            s_top = sem(name + "_top")
            width = ATT_ROW if kind == "max" else D
            used = D if kind == "edge" else D + 1
            source = att_table if kind == "max" else table

            def cols(i, k):
                return ds(i * BODY + k * PAIR, PAIR)

            def number(i, k):
                return i * SLOTS + k

            def looked(i, k):
                return 1 + i * (SLOTS + 1) + k

            def one_hots(e, i, k):
                if kind == "max" and not (isinstance(i, int) and i == 0):
                    e.wait_ge(s_seq, looked(i - 1, k + 1))
                e.wait_ge(s_pe, number(i, k) + 1)
                if kind == "first":
                    e.wait_ge(s_idx, number(i, k) + 1)
                e.tensor_tensor(onehot[:, k, :, :], iota[:, :].unsqueeze(1).broadcast_to([P, PAIR, P]),
                                dst_f[:, cols(i, k)].unsqueeze(2).broadcast_to([P, PAIR, P]), ALU.is_equal).then_inc(s_hot, 1)

            with nc.Block() as block:
                @block.gpsimd
                def _(e):
                    e.wait_ge(stored.sem, stored.at)
                    if kind == "max":
                        e.wait_ge(relay_baton.sem, relay_baton.at)

                    def gather(i):
                        for k in range(SLOTS):
                            e.wait_ge(s_idx, number(i, k) + 1)
                            e.wait_ge(s_pe if kind in ("first", "sum") else s_pre, number(i, k) + 1)
                            if kind == "max":
                                e.wait_ge(s_side[k], 16 * i + 16)
                            e.sem_inc(s_gate, 1)
                            for c in range(PAIR):
                                e.indirect_dma_start(ring[:, k, c, 0:width], None, source,
                                                     bass.IndirectOffsetOnAxis(ap=idx[:, k, c:c + 1], axis=0)).then_inc(s_got[k], 16)

                    rounds_of(e, ROUNDS, gather)

                if kind != "sum":
                    @block.sync
                    def _(e):
                        def move(i):
                            for k in range(SLOTS):
                                if kind == "max":
                                    e.wait_ge(s_got[k], 16 * PAIR * (i + 1))
                                    e.dma_start(att_rows[:, cols(i, k), :], ring[:, k, :, :]).then_inc(s_side[k], 16)
                                elif kind == "first":
                                    e.wait_ge(s_pre, number(i, k) + 1)
                                    e.dma_start(edge_in[:, k, :, :], bucketed_v[:, cols(i, k), :]).then_inc(s_side[k], 16)
                                else:
                                    e.wait_ge(s_pre, number(i, k) + 1)
                                    e.dma_start(edge_in[:, k, :, 0:D], bucketed_v[:, cols(i, k), 0:D]).then_inc(s_side[k], 16)
                        if kind == "max":
                            for k in range(SLOTS):
                                e.sem_inc(s_side[k], 16)
                        rounds_of(e, ROUNDS, move)
                        if kind == "max":
                            for k in range(SLOTS):
                                e.wait_ge(s_side[k], 16 * ROUNDS + 16)

                @block.scalar
                def _(e):
                    if kind in ("first", "max"):
                        e.sem_inc(s_pre, SLOTS)

                    def indices(i, k):
                        e.wait_ge(s_got[k], 16 * PAIR * i)
                        if kind == "first":
                            e.wait_ge(s_side[k], 16 * i + 16)
                            e.copy(dst_f[:, cols(i, k)], edge_in[:, k, :, D + 1])
                            e.copy(src_i[:, cols(i, k)], edge_in[:, k, :, D])
                            e.copy(idx[:, k, :], edge_in[:, k, :, D]).then_inc(s_idx, 1)
                            e.wait_ge(s_idx, number(i, k) + 1)
                            e.sem_inc(s_pre, 1)
                        else:
                            e.copy(idx[:, k, :], src_i[:, cols(i, k)]).then_inc(s_idx, 1)

                    def work(i, k):
                        if kind == "edge":
                            e.wait_ge(s_pre, number(i, k) + 1 + SLOTS)
                            e.activation(extra[:, k, :, :], extra[:, k, :, :], ACT.Relu).then_inc(s_msg, 1)
                        if kind == "max":
                            e.wait_ge(s_got[k], 16 * PAIR * (i + 1))
                            e.wait_ge(s_pe, number(i, k) + 1)
                            for c in range(PAIR):
                                last = e.activation(extra[:, k, c, :], ident[:, :], ACT.Copy, scale=ring[:, k, c, D + 2:D + 3])
                            last.then_inc(s_msg, 1)
                            e.copy(a_src_e[:, cols(i, k)], ring[:, k, :, D + 1]).then_inc(s_pre, 1)

                    def one(i, more=True):
                        for k in range(SLOTS):
                            work(i, k)
                            if more:
                                indices(i + 1, k)
                    for k in range(SLOTS):
                        indices(0, k)
                    rounds_of(e, ROUNDS - 1, one)
                    one(ROUNDS - 1, False)

                @block.tensor
                def _(e):
                    e.sem_inc(s_pe, SLOTS)

                    def one(i):
                        for k in range(SLOTS):
                            e.wait_ge(s_add, number(i, k) + 1)
                            e.wait_ge(s_hot, number(i, k) + 1)
                            if kind in ("max", "edge"):
                                e.wait_ge(s_msg, number(i, k) + 1)
                            if kind != "max":
                                e.wait_ge(s_got[k], 16 * PAIR * (i + 1))
                            for c in range(PAIR):
                                if kind == "max":
                                    last = e.matmul(psum[:, k, c * P:(c + 1) * P], lhsT=onehot[:, k, c, :], rhs=extra[:, k, c, :], start=True, stop=True)
                                else:
                                    rhs = extra[:, k, c, :] if kind == "edge" else ring[:, k, c, 0:used]
                                    last = e.matmul(psum[:, k, 0:used], lhsT=onehot[:, k, c, :], rhs=rhs, start=c == 0, stop=c == PAIR - 1)
                            last.then_inc(s_pe, 1)
                    rounds_of(e, ROUNDS, one)

                @block.vector
                def _(e):
                    if kind == "max":
                        e.sem_inc(s_add, SLOTS)
                    else:
                        e.memset(sums[:, :, :], 0.0).then_inc(s_add, SLOTS)
                    if kind == "edge":
                        e.sem_inc(s_pre, SLOTS)
                    if kind == "max":
                        e.sem_inc(s_top, SLOTS)
                        e.sem_inc(s_seq, 1)

                    def at_tile(view, tile, n):
                        return view[:, ds(tile, 1), 0:n].rearrange("p a n -> p (a n)")

                    def look_up(k, rows, tile, to):
                        for c in range(PAIR):
                            last = e.scalar_tensor_tensor(edge_in[:, k, c, 0:P], onehot[:, k, c, :], 1.0, at_tile(rows, tile, P),
                                                          ALU.mult, ALU.mult, accum_out=to[:, c:c + 1])
                        return last

                    def pre(i, k, tile):
                        n = number(i, k)
                        if kind == "edge":
                            e.wait_ge(s_got[k], 16 * PAIR * (i + 1))
                            e.wait_ge(s_side[k], 16 * (i + 1))
                            e.wait_ge(s_pe, n + 1)
                            e.tensor_tensor(extra[:, k, :, :], ring[:, k, :, 0:D], edge_in[:, k, :, 0:D], ALU.add).then_inc(s_pre, 1)
                        if kind == "max":
                            e.wait_ge(s_hot, n + 1)
                            if k == 0:
                                e.wait_ge(s_seq, looked(i, 0))
                            look_up(k, wide, tile, edge_m[:, 0, k, :]).then_inc(s_seq, 1)

                    def add(i, k, tile):
                        n = number(i, k)
                        e.wait_ge(s_pe, n + 1 + SLOTS)
                        if kind == "max":
                            e.wait_ge(s_top, n + 1)
                            e.tensor_reduce(pair_top[:, k:k + 1], psum[:, k, 0:PAIR * P], axis=AX.X, op=ALU.max).then_inc(s_add, 1)
                        else:
                            e.wait_ge(s_add, n + SLOTS)
                            to = at_tile(sums, tile, used)
                            e.tensor_tensor(to, to, psum[:, k, 0:used], ALU.add).then_inc(s_add, 1)

                    def merge(i, k, tile):
                        n = number(i, k)
                        e.wait_ge(s_add, n + 1 + SLOTS)
                        e.wait_ge(s_top, n + SLOTS)
                        to = s["amax"][:, ds(tile, 1)]
                        e.tensor_tensor(to, to, pair_top[:, k:k + 1], ALU.max).then_inc(s_top, 1)

                    def one(i, more=True):
                        _, tile = nc.values_load_multi_w_load_instructions(
                            tile_i[0:1, ds(i * SLOTS, SLOTS)], engines=(mybir.EngineType.DVE,), min_val=0, max_val=TILES - 1,
                            skip_runtime_bounds_check_because="number of the 49 buckets that start at or before a pair, less one")
                        for k in range(SLOTS + 1):
                            if k < SLOTS:
                                pre(i, k, tile[k])
                            if k > 0:
                                add(i, k - 1, tile[k - 1])
                                if more:
                                    one_hots(e, i + 1, k - 1)
                            if k > 1 and kind == "max":
                                merge(i, k - 2, tile[k - 2])
                        if kind == "max":
                            e.wait_ge(s_seq, looked(i, SLOTS))
                            e.tensor_copy(a_dst_e[:, ds(i * BODY, BODY)], edge_m[:, 0, :, :].rearrange("p k c -> p (k c)")).then_inc(s_seq, 1)
                            merge(i, SLOTS - 1, tile[SLOTS - 1])
                    for k in range(SLOTS):
                        one_hots(e, 0, k)
                    rounds_of(e, ROUNDS - 1, one)
                    one(ROUNDS - 1, False)

        pair_top = sb("pair_top", [P, SLOTS])
        edge_w, edge_m, edge_d = (sb(n, [P, 2, SLOTS, PAIR]) for n in ("edge_w", "edge_m", "edge_d"))

        def weigh_pass():
            s_got = [sem(f"weigh_got{k}") for k in range(SLOTS)]
            s_dst = sem("weigh_dst")
            s_sub = sem("weigh_sub")
            s_exp = sem("weigh_exp")
            s_hot_p, s_hot_v = sem("weigh_hot_p"), sem("weigh_hot_v")
            s_pe = sem("weigh_pe")
            s_add = sem("weigh_add")
            s_look = sem("weigh_look")
            chunks = [(k, c) for k in range(SLOTS) for c in range(PAIR)]
            by_pool, by_vector = chunks[:5], chunks[5:]
            assert ROUNDS % 2 == 0

            def weighted(e, h, k, c):
                return e.tensor_scalar(onehot[:, k, c, :], iota[:, :], edge_d[:, h, k, c:c + 1], edge_w[:, h, k, c:c + 1],
                                       op0=ALU.is_equal, op1=ALU.mult)

            def made(mine, r, k):
                return len(mine) * r + sum(slot <= k for slot, _ in mine)

            with nc.Block() as block:
                @block.sync
                def _(e):
                    def load(i):
                        for k in range(SLOTS):
                            e.wait_ge(s_pe, SLOTS * i + k + 1)
                            e.dma_start(ring[:, k, :, :], att_rows[:, ds(i * BODY + k * PAIR, PAIR), :]).then_inc(s_got[k], 16)
                    rounds_of(e, ROUNDS, load)

                @block.scalar
                def _(e):
                    def fetch(r, h):
                        e.wait_ge(s_pe, SLOTS * r)
                        e.copy(edge_d[:, h, :, :].rearrange("p k c -> p (k c)"), dst_f[:, ds(r * BODY, BODY)]).then_inc(s_dst, 1)

                    def one(i, more=True):
                        for h in range(2):
                            r = 2 * i + h
                            e.wait_ge(s_sub, r + 1)
                            e.activation(edge_w[:, h, :, :], edge_w[:, h, :, :], ACT.Exp).then_inc(s_exp, 1)
                            if more or h == 0:
                                fetch(r + 1, 1 - h)
                    fetch(0, 0)
                    rounds_of(e, ROUNDS // 2 - 1, one)
                    one(ROUNDS // 2 - 1, False)

                @block.gpsimd
                def _(e):
                    def one(i):
                        for h in range(2):
                            r = 2 * i + h
                            e.wait_ge(s_exp, r + 1)
                            for k, c in by_pool:
                                e.wait_ge(s_pe, SLOTS * r + k + 1)
                                e.sem_inc(s_gate, 1)
                                weighted(e, h, k, c).then_inc(s_hot_p, 1)
                    rounds_of(e, ROUNDS // 2, one)

                @block.tensor
                def _(e):
                    e.sem_inc(s_pe, SLOTS)

                    def one(i):
                        for k in range(SLOTS):
                            e.wait_ge(s_add, SLOTS * i + k + 1)
                            for hot, mine in ((s_hot_p, by_pool), (s_hot_v, by_vector)):
                                if any(slot == k for slot, _ in mine):
                                    e.wait_ge(hot, made(mine, i, k))
                            e.wait_ge(s_got[k], 16 * i + 16)
                            for c in range(PAIR):
                                last = e.matmul(psum[:, k, 0:D + 1], lhsT=onehot[:, k, c, :], rhs=ring[:, k, c, 0:D + 1], start=c == 0, stop=c == PAIR - 1)
                            last.then_inc(s_pe, 1)
                    rounds_of(e, ROUNDS, one)

                @block.vector
                def _(e):
                    e.memset(sums[:, :, :], 0.0).then_inc(s_add, SLOTS)

                    def load_tiles(first, n):
                        return nc.values_load_multi_w_load_instructions(
                            tile_i[0:1, ds(first, n)], engines=(mybir.EngineType.DVE,), min_val=0, max_val=TILES - 1,
                            skip_runtime_bounds_check_because="number of the 49 buckets that start at or before a pair, less one")[1]

                    def look_up(r, h, k, tile):
                        for c in range(PAIR):
                            last = e.scalar_tensor_tensor(edge_in[:, k, c, 0:P], iota[:, :], edge_d[:, h, k, c:c + 1],
                                                          wide2[:, ds(tile, 1), :].rearrange("p a n -> p (a n)"),
                                                          ALU.is_equal, ALU.mult, accum_out=edge_m[:, h, k, c:c + 1])
                        return last

                    def subtract(r, h):
                        e.wait_ge(s_look, r + 1)
                        e.tensor_tensor(edge_w[:, h, :, :].rearrange("p k c -> p (k c)"), a_src_e[:, ds(r * BODY, BODY)],
                                        edge_m[:, h, :, :].rearrange("p k c -> p (k c)"), ALU.subtract).then_inc(s_sub, 1)

                    def weigh(r, h):
                        e.wait_ge(s_exp, r + 1)
                        for k, c in by_vector:
                            e.wait_ge(s_pe, SLOTS * r + k + 1)
                            weighted(e, h, k, c).then_inc(s_hot_v, 1)

                    def add(r, k, tile):
                        n = SLOTS * r + k
                        e.wait_ge(s_pe, n + 1 + SLOTS)
                        e.wait_ge(s_add, n + SLOTS)
                        to = sums[:, ds(tile, 1), 0:D + 1].rearrange("p a n -> p (a n)")
                        e.tensor_tensor(to, to, psum[:, k, 0:D + 1], ALU.add).then_inc(s_add, 1)

                    def one(i, first=False, last=False):
                        tile = load_tiles(0, 3 * SLOTS) if first else load_tiles((2 * i - 1) * SLOTS, 4 * SLOTS)
                        before = 0 if first else SLOTS
                        for h in range(2):
                            r = 2 * i + h
                            weigh(r, h)
                            ahead = not (last and h == 1)
                            if ahead:
                                e.wait_ge(s_dst, r + 2)
                            for k in range(SLOTS):
                                if ahead:
                                    seen = look_up(r + 1, 1 - h, k, tile[before + SLOTS * (h + 1) + k])
                                if not (first and h == 0):
                                    add(r - 1, k, tile[before + SLOTS * (h - 1) + k])
                            if ahead:
                                seen.then_inc(s_look, 1)
                                subtract(r + 1, 1 - h)
                    tile = load_tiles(0, SLOTS)
                    e.wait_ge(s_dst, 1)
                    for k in range(SLOTS):
                        seen = look_up(0, 0, k, tile[k])
                    seen.then_inc(s_look, 1)
                    subtract(0, 0)
                    one(0, first=True)
                    with e.Fori(1, ROUNDS // 2 - 1) as i:
                        one(i)
                    one(ROUNDS // 2 - 1, last=True)
                    tile = load_tiles((ROUNDS - 1) * SLOTS, SLOTS)
                    for k in range(SLOTS):
                        add(ROUNDS - 1, k, tile[k])

        layer_norm(store=True)
        edge_pass("gin", "first")
        counts = sums[:, :, D]
        run([("vector", lambda e, _: e.tensor_scalar(s["rcount"][:, :], counts, 1.0, None, op0=ALU.max), 1),
             ("vector", lambda e, _: e.reciprocal(s["rcount"][:, :], s["rcount"][:, :]), 1),
             ("vector", lambda e, _: e.tensor_tensor(s["some"][:, :], s["rcount"][:, :], counts, ALU.mult), 1)])
        by_feature = wide[:, :, :].rearrange("p i n -> p (i n)")
        split = BATCH * D // 2

        def mlp_product(w, k):
            def emit(e, i):
                src = turned[0][:, :, :].rearrange("p t n -> p (t n)") if k == 1 else stage[1][:, :, :].rearrange("p t n -> p (t n)")
                for m in range(2):
                    last = e.matmul(psum[:, 2 * k + m, 0:split], lhsT=w[:, :], rhs=src[:, m * split:(m + 1) * split], start=True, stop=True)
                return last
            return emit

        def halves(view):
            return view.rearrange("p (m n) -> p m n", m=2)
        run([
            ("vector", lambda e, i: e.tensor_tensor(stage[0][:, :, :], batch(h, i), batch(sums, i)[:, :, 0:D], ALU.add), 1),
            ("tensor", turn(stage[0], 0), 1),
            ("scalar", lambda e, i: e.copy(turned[0][:, :, :], batch_psum(0)), 1),
            ("tensor", mlp_product(W["L0_gnn_W1"], 1), 1),
            ("scalar", lambda e, i: e.activation(halves(stage[1][:, :, :].rearrange("p t n -> p (t n)")), psum[:, 2:4, 0:split], ACT.Relu,
                                                 bias=col["L0_gnn_b1"][:, :]), 1),
            ("tensor", mlp_product(W["L0_gnn_W2"], 2), 1),
            ("scalar", lambda e, i: e.activation(halves(by_feature[:, ds(i * BATCH * D, BATCH * D)]), psum[:, 4:6, 0:split], ACT.Relu,
                                                 bias=col["L0_gnn_b2"][:, :]), 1),
        ], BATCHES)
        pieces = [(a, min(512, N_NODES - a)) for a in range(0, N_NODES, 512)]

        def column_stats(e, _):
            for k, (a, n) in enumerate(pieces):
                last = e.bn_stats(moments[:, k, :], by_feature[:, a:a + n])
            return last
        scale_c, shift_c = sb("scale_c", [P, 1]), sb("shift_c", [P, 1])
        run([("vector", column_stats, 1),
             ("vector", lambda e, _: e.bn_aggr(mean_var[:, 0, :], moments[:, 0:len(pieces), :].rearrange("p k s -> p (k s)")), 1),
             ("scalar", lambda e, _: e.activation(scale_c[:, :], mean_var[:, 0, 1:2], ACT.Sqrt, bias=eps[:, :]), 1),
             ("vector", lambda e, _: e.reciprocal(scale_c[:, :], scale_c[:, :]), 1),
             ("vector", lambda e, _: e.tensor_tensor(scale_c[:, :], scale_c[:, :], col["L0_gnn_gamma"][:, :], ALU.mult), 1)])
        run([
            ("vector", lambda e, i: e.tensor_scalar(stage[0][:, :, :].rearrange("p t n -> p (t n)"), by_feature[:, ds(i * BATCH * D, BATCH * D)],
                                                    mean_var[:, 0, 0:1], scale_c[:, 0:1], op0=ALU.subtract, op1=ALU.mult), 1),
            ("scalar", lambda e, i: e.activation(stage[1][:, :, :], stage[0][:, :, :], ACT.Identity, bias=col["L0_gnn_beta"][:, :]), 1),
            ("tensor", turn(stage[1], 0), 1),
            ("vector", lambda e, i: e.tensor_tensor(batch(x, i), batch(x, i), batch_psum(0), ALU.add), 1),
        ], BATCHES)

        layer_norm(store=False)
        run([("vector", lambda e, _: e.memset(sums[:, :, D + 3:ROW], 0.0), 1)])

        def att(name, to):
            def product(e, i, p):
                return e.tensor_tensor(stage[1][:, :, :], batch(sums, i)[:, :, 0:D], row[name][:, :].unsqueeze(1).broadcast_to(tiles(BATCH)), ALU.mult)

            def total(e, i, p):
                return e.tensor_reduce(s[to][:, ds(i * BATCH, BATCH)], stage[1][:, :, :], axis=AX.X, op=ALU.add)
            return [("vector", product), ("vector", total)]
        dense([(*nodes_of(h), W["L1_gnn_W"])],
              [("scalar", lambda e, i, p: e.copy(batch(sums, i)[:, :, 0:D], p))] + att("L1_gnn_att_src", "a_src") + att("L1_gnn_att_dst", "a_dst"))
        least, low = sb("least", [P, 1]), sb("low", [P, 1])
        run([("vector", lambda e, _: e.tensor_reduce(least[:, :], s["a_src"][:, :], axis=AX.X, op=ALU.min), 1),
             ("tensor", lambda e, _: e.transpose(flat[0:1, 0:P], least[:, :], ident[:, :]), 1),
             ("vector", lambda e, _: e.tensor_reduce(junk[0:1, 0:1], flat[0:1, 0:P], axis=AX.X, op=ALU.min), 1),
             ("tensor", lambda e, _: e.matmul(flat[:, 512:513], lhsT=ones[0:1, :], rhs=junk[0:1, 0:1], start=True, stop=True), 1),
             ("vector", lambda e, _: e.tensor_copy(low[:, :], flat[:, 512:513]), 1),
             ("vector", lambda e, _: e.memset(sums[:, :, D:D + 1], 1.0), 1),
             ("vector", lambda e, _: e.tensor_copy(sums[:, :, D + 1], s["a_src"][:, :]), 1),
             ("vector", lambda e, _: e.tensor_scalar(sums[:, :, D + 2], s["a_src"][:, :], low[:, 0:1], None, op0=ALU.subtract), 1),
             ("sync", lambda e, _: e.dma_start(att_table.rearrange("(i p) w -> p i w", p=P), sums[:, :, :]), 16),
             ("vector", lambda e, _: e.memset(s["amax"][:, :], 0.0), 1)])
        on_every_partition(s["a_dst"], wide)
        edge_pass("att_max", "max")
        run([("vector", lambda e, _: e.scalar_tensor_tensor(s["top"][:, :], s["amax"][:, :], low[:, 0:1], s["a_dst"][:, :], ALU.add, ALU.add), 1),
             ("vector", lambda e, _: e.scalar_tensor_tensor(s["mean"][:, :], s["top"][:, :], SLOPE, s["top"][:, :], ALU.mult, ALU.max), 1)])
        on_every_partition(s["mean"], wide2)
        run([("vector", lambda e, _: e.tensor_tensor(a_src_e[:, :], a_src_e[:, :], a_dst_e[:, :], ALU.add), 1),
             ("vector", lambda e, _: e.scalar_tensor_tensor(a_src_e[:, :], a_src_e[:, :], SLOPE, a_src_e[:, :], ALU.mult, ALU.max), 1)])
        weigh_pass()
        run([("vector", lambda e, _: e.tensor_scalar(s["rden"][:, :], sums[:, :, D], 1e-16, None, op0=ALU.add), 1),
             ("vector", lambda e, _: e.reciprocal(s["rden"][:, :], s["rden"][:, :]), 1),
             ("vector", lambda e, _: e.tensor_tensor(h[:, :, :], sums[:, :, 0:D], s["rden"][:, :].unsqueeze(2).broadcast_to(tiles()), ALU.mult), 1),
             ("vector", lambda e, _: e.tensor_tensor(h[:, :, :], h[:, :, :], row["L1_gnn_bias"][:, :].unsqueeze(1).broadcast_to(tiles()), ALU.add), 1),
             ("vector", lambda e, _: e.scalar_tensor_tensor(x[:, :, :].rearrange("p i f -> p (i f)"), h[:, :, :].rearrange("p i f -> p (i f)"), 0.0,
                                                            x[:, :, :].rearrange("p i f -> p (i f)"), ALU.max, ALU.add), 1)])

        layer_norm(store=True)
        for n in (1, 2, 3):
            edge_pass(f"sage{n}", "sum")
            finish = [("vector", plus_row(f"L2_gnn_b{n}", lambda i: batch(h, i)))]
            if n == 1:
                finish.append(("scalar", lambda e, i, p: e.activation(batch(h, i), batch(h, i), ACT.Relu)))
            if n == 3:
                finish.append(("vector", lambda e, i, p: e.tensor_tensor(batch(x, i), batch(x, i), batch(h, i), ALU.add)))
            dense([(*mean_of_sums(), W[f"L2_gnn_Wl{n}"]), (*nodes_of(h), W[f"L2_gnn_Wr{n}"])], finish, store=h if n < 3 else None)

        layer_norm(store=False)
        dense([(*nodes_of(h), W["node"])], [("vector", plus_row("L3_gnn_b1a", lambda i: batch(wide, i)))], store=wide)
        edge_pass("meta", "edge")
        dense([(*mean_of_sums(), W["L3_gnn_W1b"])],
              [("vector", lambda e, i, p: e.tensor_tensor(stage[1][:, :, :], row["L3_gnn_b1b"][:, :].unsqueeze(1).broadcast_to(tiles(BATCH)),
                                                          s["some"][:, ds(i * BATCH, BATCH)].unsqueeze(2).broadcast_to(tiles(BATCH)), ALU.mult)),
               ("vector", lambda e, i, p: e.tensor_tensor(batch(wide, i), stage[1][:, :, :], p, ALU.add))], reader=1)
        run([("vector", lambda e, _: e.tensor_copy(junk[0:D_EDGE, :], u0[:, :].broadcast_to([D_EDGE, P])), 1),
             ("tensor", lambda e, _: e.matmul(flat[:, 0:D], lhsT=junk[0:D_EDGE, :], rhs=W["u"][:, :], start=True, stop=True), 1),
             ("vector", lambda e, _: e.tensor_tensor(row["L3_gnn_b2a"][:, :], row["L3_gnn_b2a"][:, :], flat[:, 0:D], ALU.add), 1)])
        dense([(*nodes_of(h), W["h"]), ("vector", lambda e, i, out: e.tensor_copy(out[:, :, :], batch(wide, i)), W["agg"])],
              [("vector", plus_row("L3_gnn_b2a", lambda i: batch(wide2, i))),
               ("scalar", lambda e, i, p: e.activation(batch(wide2, i), batch(wide2, i), ACT.Relu))])
        dense([(*nodes_of(wide2), W["L3_gnn_W2b"])],
              [("vector", plus_row("L3_gnn_b2b", lambda i: batch(wide2, i))),
               ("vector", lambda e, i, p: e.tensor_tensor(batch(x, i), batch(x, i), batch(wide2, i), ALU.add))])
        s_out = sem("s_out")

        def store(e, _):
            e.dma_start(out[0:full_nodes * P, :].rearrange("(i p) f -> p i f", p=P), x[:, 0:full_nodes, :]).then_inc(s_out, 16)
            e.dma_start(out[full_nodes * P:N_NODES, :], x[0:N_NODES - full_nodes * P, full_nodes, :]).then_inc(s_out, 16)
            e.wait_ge(s_out, 32)
            return e.nop()
        run([("sync", store, 1)])


def kernel(**inputs):
    import numpy as np
    import concourse.bacc as bacc
    from concourse.bass_utils import run_bass_kernel_spmd as launch

    a = {k: np.ascontiguousarray(v) for k, v in inputs.items()}
    for n in (1, 2, 3):
        for side in "lr":
            a[f"L2_gnn_W{side}{n}"] = np.ascontiguousarray(a[f"L2_gnn_W{side}{n}"].T)
    for name in ("src", "dst"):
        v = a.pop(name)
        a[name + "_full"] = np.ascontiguousarray(v[:FULL_IN * P].reshape(FULL_IN, P).T)
        a[name + "_tail"] = np.ascontiguousarray(v[FULL_IN * P:].reshape(TAIL_IN, 1))
    a["attr_t"] = np.ascontiguousarray(a.pop("edge_attr_64").T)
    nc = bacc.Bacc("TRN2", target_bir_lowering=False, num_devices=1)
    t = {k: nc.dram_tensor("in_" + k, v.shape, mybir.dt.from_np(v.dtype), kind="ExternalInput").ap() for k, v in a.items()}
    out = nc.dram_tensor("out", (N_NODES, D), fp32, kind="ExternalOutput").ap()
    build(nc, t, out)
    r = launch(nc, [{"in_" + k: v for k, v in a.items()}], core_ids=[0])
    return r.results[0]["out"]
```
